# Optimizing a Trainium2 kernel written in Bass

```python
import numpy as np
import jax
import jax.numpy as jnp

def _softmax(x, axis=-1):
    return jax.nn.softmax(x, axis=axis)

def _gelu(x):
    return jax.nn.gelu(x, approximate=True)

def _silu(x):
    return jax.nn.silu(x)

def _sigmoid(x):
    return jax.nn.sigmoid(x)

def _layernorm(x, axis=-1, eps=1e-05):
    m = jnp.mean(x, axis=axis, keepdims=True)
    v = jnp.var(x, axis=axis, keepdims=True)
    return (x - m) / jnp.sqrt(v + eps)

def _scatter_add(tgt, idx, src, axis=0):
    return tgt.at[idx].add(src)

def _segment_sum(src, seg, n):
    return jax.ops.segment_sum(src, seg, n)
kernel_name = 'mk_seq_postln_d1_jaxref_r4_c2e77e'

def setup_inputs(seed: int=0):
    np.random.seed(seed)
    _w = jnp.asarray

    def _L0_attn_setup():
        import jax, jax.numpy as jnp
        import numpy as np
        D_MODEL = 256
        N_HEADS = 16
        HEAD_DIM = D_MODEL // N_HEADS
        BATCH = 2
        SEQ = 512

        def _alibi_bias(seq_len, n_heads, dtype):
            slopes = 1.0 / 2.0 ** (jnp.arange(n_heads, dtype=dtype) / n_heads)
            rel = jnp.arange(seq_len, dtype=dtype)[None, :] - jnp.arange(seq_len, dtype=dtype)[:, None]
            return slopes[:, None, None] * rel[None, :, :]
        key = jax.random.key(seed)
        ks = jax.random.split(key, 9)
        s = 0.02
        return {'x': jax.random.normal(ks[0], (BATCH, SEQ, D_MODEL), dtype=jnp.float32), 'Wq': jax.random.normal(ks[1], (D_MODEL, D_MODEL), dtype=jnp.float32) * s, 'bq': jnp.zeros((D_MODEL,), dtype=jnp.float32), 'Wk': jax.random.normal(ks[2], (D_MODEL, D_MODEL), dtype=jnp.float32) * s, 'bk': jnp.zeros((D_MODEL,), dtype=jnp.float32), 'Wv': jax.random.normal(ks[3], (D_MODEL, D_MODEL), dtype=jnp.float32) * s, 'bv': jnp.zeros((D_MODEL,), dtype=jnp.float32), 'Wo': jax.random.normal(ks[4], (D_MODEL, D_MODEL), dtype=jnp.float32) * s, 'bo': jnpp_zeros() if False else jnp.zeros((D_MODEL,), dtype=jnp.float32)}
    _L0_attn_in = _L0_attn_setup()

    def _L0_ffn_setup():
        import jax, jax.numpy as jnp
        import numpy as np
        D_MODEL, D_FF, RANK = (256, 1024, 64)
        B, S = (4, 1024)
        key = jax.random.key(seed)
        ks = jax.random.split(key, 7)
        return {'x': jax.random.normal(ks[0], (B, S, D_MODEL), dtype=jnp.float32), 'U1': jax.random.normal(ks[1], (D_MODEL, RANK), dtype=jnp.float32) * 0.02, 'V1': jax.random.normal(ks[2], (RANK, D_FF), dtype=jnp.float32) * 0.02, 'b1': jnp.zeros((D_FF,), dtype=jnp.float32), 'U2': jax.random.normal(ks[3], (D_FF, RANK), dtype=jnp.float32) * 0.02, 'V2': jax.random.normal(ks[4], (RANK, D_MODEL), dtype=jnp.float32) * 0.02, 'b2': jnp.zeros((D_MODEL,), dtype=jnp.float32)}
    _L0_ffn_in = _L0_ffn_setup()
    _d = {'L0_attn_x': _L0_attn_in['x'], 'L0_attn_Wq': _L0_attn_in['Wq'], 'L0_attn_bq': _L0_attn_in['bq'], 'L0_attn_Wk': _L0_attn_in['Wk'], 'L0_attn_bk': _L0_attn_in['bk'], 'L0_attn_Wv': _L0_attn_in['Wv'], 'L0_attn_bv': _L0_attn_in['bv'], 'L0_attn_Wo': _L0_attn_in['Wo'], 'L0_attn_bo': _L0_attn_in['bo'], 'L0_ffn_U1': _L0_ffn_in['U1'], 'L0_ffn_V1': _L0_ffn_in['V1'], 'L0_ffn_b1': _L0_ffn_in['b1'], 'L0_ffn_U2': _L0_ffn_in['U2'], 'L0_ffn_V2': _L0_ffn_in['V2'], 'L0_ffn_b2': _L0_ffn_in['b2']}
    _x0 = _d['L0_attn_x']
    _d['L0_attn_x'] = jax.random.normal(jax.random.fold_in(jax.random.key(seed), 1), (4, 2048, 256), dtype=_x0.dtype)
    del _x0
    return _d

def reference(L0_attn_x, L0_attn_Wq, L0_attn_bq, L0_attn_Wk, L0_attn_bk, L0_attn_Wv, L0_attn_bv, L0_attn_Wo, L0_attn_bo, L0_ffn_U1, L0_ffn_V1, L0_ffn_b1, L0_ffn_U2, L0_ffn_V2, L0_ffn_b2):

    def _L0_attn_ref(x, Wq, bq, Wk, bk, Wv, bv, Wo, bo):
        import jax, jax.numpy as jnp
        import numpy as np
        D_MODEL = 256
        N_HEADS = 16
        HEAD_DIM = D_MODEL // N_HEADS
        BATCH = 2
        SEQ = 512

        def _alibi_bias(seq_len, n_heads, dtype):
            slopes = 1.0 / 2.0 ** (jnp.arange(n_heads, dtype=dtype) / n_heads)
            rel = jnp.arange(seq_len, dtype=dtype)[None, :] - jnp.arange(seq_len, dtype=dtype)[:, None]
            return slopes[:, None, None] * rel[None, :, :]
        B, S, D = x.shape
        H, Hd = (N_HEADS, HEAD_DIM)
        scale = Hd ** (-0.5)
        Q = (x @ Wq + bq).reshape(B, S, H, Hd)
        K = (x @ Wk + bk).reshape(B, S, H, Hd)
        V = (x @ Wv + bv).reshape(B, S, H, Hd)
        scores = jnp.einsum('bqhd,bkhd->bhqk', Q, K) * scale
        scores = scores + _alibi_bias(S, H, x.dtype)[None]
        attn = jax.nn.softmax(scores, axis=-1)
        out = jnp.einsum('bhqk,bkhd->bqhd', attn, V).reshape(B, S, D)
        return out @ Wo + bo

    def _L0_ffn_ref(x, U1, V1, b1, U2, V2, b2):
        import jax, jax.numpy as jnp
        import numpy as np
        D_MODEL, D_FF, RANK = (256, 1024, 64)
        B, S = (4, 1024)
        P = jnp.einsum('bsd,dr->bsr', x, U1)
        H = jax.nn.gelu(jnp.einsum('bsr,rf->bsf', P, V1) + b1)
        Q = jnp.einsum('bsf,fr->bsr', H, U2)
        return jnp.einsum('bsr,rd->bsd', Q, V2) + b2
    x = L0_attn_x
    x = _layernorm(x + _L0_attn_ref(x, L0_attn_Wq, L0_attn_bq, L0_attn_Wk, L0_attn_bk, L0_attn_Wv, L0_attn_bv, L0_attn_Wo, L0_attn_bo), axis=-1)
    x = _layernorm(x + _L0_ffn_ref(x, L0_ffn_U1, L0_ffn_V1, L0_ffn_b1, L0_ffn_U2, L0_ffn_V2, L0_ffn_b2), axis=-1)
    return x

_drawn_inputs = setup_inputs


def setup_inputs(seed=0):
    import zlib

    import numpy as np

    out = dict(_drawn_inputs(seed))
    spreads = {'L0_attn_bq': (0.0, 0.8),
     'L0_attn_bk': (0.0, 2.0),
     'L0_attn_bv': (0.0, 0.304),
     'L0_attn_bo': (0.0, 0.1),
     'L0_ffn_b1': (0.0, 0.8),
     'L0_ffn_b2': (0.0, 0.8)}
    factors = {'L0_attn_Wq': 8.0,
     'L0_attn_Wk': 8.0,
     'L0_ffn_U1': 8.0,
     'L0_ffn_V1': 8.0,
     'L0_ffn_U2': 8.0,
     'L0_ffn_V2': 8.0}
    for name, (base, spread) in spreads.items():
        noise = np.random.default_rng([zlib.crc32(name.encode()), seed]).standard_normal(out[name].shape)
        drawn = base * np.exp(spread * noise) if base else spread * noise
        out[name] = jnp.asarray(drawn.astype(out[name].dtype))
    for name, factor in factors.items():
        out[name] = (out[name] * factor).astype(out[name].dtype)
    return out
```

```python
from contextlib import ExitStack

import numpy as np

import concourse.bass as bass
from concourse import mybir

F32 = mybir.dt.float32
BF16 = mybir.dt.bfloat16
ALU = mybir.AluOpType
ACT = mybir.ActivationFunctionType
AX = mybir.AxisListType

P = 128
B, S, D = 4, 2048, 256
H = 16
HD = D // H
BH = B * H
KC = D // P
HH = H // KC
NT = S // P
N = 512
NB = S // N
FF, RANK = 1024, 64
EPS = 1e-5
SCALE = float(HD) ** -0.5
PARTS = 3
SPLIT_ROWS = PARTS * HD + PARTS
VW = 2 * HD


def split_constant(x):
    parts, rest = [], x.astype(np.float32)
    for _ in range(PARTS):
        part = rest.astype(mybir.dt.np(BF16))
        parts.append(part)
        rest = rest - part.astype(np.float32)
    return np.stack(parts, axis=-2)


def alibi_rows():
    slopes = (1.0 / 2.0 ** (np.arange(H, dtype=np.float32) / H)).astype(np.float32)
    ramp = slopes[:, None] * np.arange(S, dtype=np.float32)[None, :]
    return split_constant(ramp), split_constant(-ramp)


def project_and_split(nc, x, weights, biases, alibi_k, alibi_q, k_parts, q_parts, v_rows, identity_in):
    names = ("q", "k")
    with ExitStack() as ctx:
        def sb(name, shape, dt=F32):
            return ctx.enter_context(nc.sbuf_tensor("a_" + name, shape, dt))

        def sem(name):
            return ctx.enter_context(nc.semaphore("a_" + name))

        ident = sb("ident", [P, P])
        w_sb = {n: sb("w" + n, [P, KC, D]) for n in "qkv"}
        bias_col = {n: sb("bias_" + n, [P, KC]) for n in names}
        bq_scaled = sb("bq_scaled", [P, KC])
        bv_rows = sb("bv_rows", [P, D])
        x_sb = sb("x", [P, NT, D])
        xT = sb("xT", [P, KC, S])
        full = sb("full", [P, 2, N])
        rest = sb("rest", [P, 2, N])
        parts = {n: sb("parts_" + n, [P, KC, PARTS, S], BF16) for n in names}
        v_sb = sb("v", [P, H, NT, VW])
        banks = [ctx.enter_context(nc.psum_tensor(f"a_bank{i}", [P, N], F32)) for i in range(8)]

        constants_in = sem("constants_in")
        x_in = sem("x_in")
        bias_scaled = sem("bias_scaled")
        ones_set = sem("ones_set")
        transposed = sem("transposed")
        xT_ready = sem("xT_ready")
        projected = sem("projected")
        part1_out = sem("part1_out")
        rest_ready = sem("rest_ready")
        part2_out = sem("part2_out")
        split_seen = sem("split_seen")
        split_done = sem("split_done")
        v_projected = sem("v_projected")
        v_ready = sem("v_ready")
        parts_stored = sem("parts_stored")
        v_stored = sem("v_stored")
        alibi_stored = sem("alibi_stored")

        XG = KC * NB
        QK = 2 * KC * NB
        VG = NT // 2
        tiles = [(n, c, j) for j in range(NB) for n in range(2) for c in range(KC)]
        stores = 2 * KC * PARTS

        block = ctx.enter_context(nc.Block())

        @block.sync
        def _(sp):
            sp.dma_start(ident[:, :], identity_in).then_inc(constants_in, 16)
            for n in "qkv":
                sp.dma_start(w_sb[n][:, :, :], weights[n].rearrange("(c p) n -> p c n", p=P)).then_inc(constants_in, 16)
            for n in names:
                sp.dma_start(bias_col[n][:, :], biases[n].rearrange("(c p) -> p c", p=P),
                             allow_slow_non_contiguous=True).then_inc(constants_in, 16)
            sp.dma_start(bv_rows[:, :], biases["v"].partition_broadcast(P)).then_inc(constants_in, 16)
            with sp.Fori(0, B) as b:
                sp.wait_ge(transposed, b * XG + 1)
                sp.dma_start(x_sb[:, :, :], x[bass.ds(b, 1), :, :].rearrange("a (t p) d -> p (a t) d", p=P)).then_inc(x_in, 16)
                for src, dst in ((alibi_q, q_parts), (alibi_k, k_parts)):
                    sp.dma_start(dst[bass.ds(b * H, H), PARTS * HD:SPLIT_ROWS, :], src).then_inc(alibi_stored, 16)
                sp.wait_ge(split_done, b * QK + QK)
                sp.sem_inc(split_seen, 1)
                for n, dst in ((0, q_parts), (1, k_parts)):
                    for c in range(KC):
                        for j in range(PARTS):
                            sp.dma_start(dst[bass.ds(b * H + c * HH, HH), j * HD:(j + 1) * HD, :],
                                         parts[names[n]][:, c, j, :]).then_inc(parts_stored, 16)
                sp.wait_ge(v_ready, b * VG + VG + 1)
                sp.dma_start(v_rows[bass.ds(b * H, H), :, :].rearrange("h p n -> p h n"),
                             v_sb[:, :, :, :].rearrange("p h t w -> p h (t w)")).then_inc(v_stored, 16)
            sp.wait_ge(parts_stored, 16 * stores * B + 16)
            sp.wait_ge(v_stored, 16 * B + 16)
            sp.wait_ge(alibi_stored, 32 * B)

        @block.tensor
        def _(pe):
            pe.sem_inc(transposed, 1)
            pe.wait_ge(constants_in, 16 * 7)
            with pe.Fori(0, B) as b:
                pe.wait_ge(x_in, b * 16 + 16)
                g = 0
                for j in range(NB):
                    for c in range(KC):
                        pe.wait_ge(v_ready, b * VG + 1)
                        for i in range(NB):
                            last = nc.tensor.transpose(banks[g][:, i * P:(i + 1) * P],
                                                       x_sb[:, j * 4 + i, c * P:(c + 1) * P], ident[:, :])
                        last.then_inc(transposed, 1)
                        g += 1
                pe.wait_ge(xT_ready, b * XG + XG)
                for i, (n, c, j) in enumerate(tiles):
                    if i >= 8:
                        pe.wait_ge(part1_out, b * QK + i - 7)
                    for h in range(KC):
                        last = nc.tensor.matmul(banks[i % 8][:, :], w_sb[names[n]][:, h, c * P:(c + 1) * P],
                                                xT[:, h, j * N:(j + 1) * N], start=(h == 0), stop=(h == KC - 1))
                    last.then_inc(projected, 1)
                for i in range(VG):
                    pe.wait_ge(part1_out, b * QK + QK - 7 + i)
                    for t in range(2):
                        for h in range(KC):
                            last = nc.tensor.matmul(banks[i % 8][:, t * D:(t + 1) * D],
                                                    xT[:, h, (2 * i + t) * P:(2 * i + t + 1) * P], w_sb["v"][:, h, :],
                                                    start=(h == 0), stop=(h == KC - 1))
                    last.then_inc(v_projected, 1)

        @block.scalar
        def _(act):
            act.sem_inc(parts_stored, 16)
            act.wait_ge(constants_in, 16 * 7)
            nc.scalar.mul(bq_scaled[:, :], bias_col["q"][:, :], SCALE).then_inc(bias_scaled, 1)
            act.wait_ge(bias_scaled, 1)
            with act.Fori(0, B) as b:
                act.wait_ge(parts_stored, b * (16 * stores) + 16)
                for i, (n, c, j) in enumerate(tiles):
                    act.wait_ge(projected, b * QK + (i + 1))
                    if i >= 2:
                        act.wait_ge(split_done, b * QK + (i - 1))
                    bias = bq_scaled if n == 0 else bias_col["k"]
                    scale = SCALE if n == 0 else 1.0
                    nc.scalar.activation(full[:, i % 2, :], banks[i % 8][:, :], ACT.Identity,
                                         bias=bias[:, c:c + 1], scale=scale)
                    nc.scalar.activation(parts[names[n]][:, c, 0, j * N:(j + 1) * N], banks[i % 8][:, :], ACT.Identity,
                                         bias=bias[:, c:c + 1], scale=scale).then_inc(part1_out, 1)

        @block.vector
        def _(dve):
            dve.sem_inc(v_ready, 1)
            dve.sem_inc(v_stored, 16)
            nc.vector.memset(v_sb[:, :, :, :], 1.0).then_inc(ones_set, 1)
            dve.wait_ge(ones_set, 1)
            dve.wait_ge(constants_in, 16 * 7)
            with dve.Fori(0, B) as b:
                g = 0
                for j in range(NB):
                    for c in range(KC):
                        dve.wait_ge(transposed, b * XG + (g + 2))
                        nc.vector.tensor_copy(xT[:, c, j * N:(j + 1) * N], banks[g][:, :]).then_inc(xT_ready, 1)
                        g += 1
                for i, (n, c, j) in enumerate(tiles):
                    dst = parts[names[n]]
                    cols = slice(j * N, (j + 1) * N)
                    dve.wait_ge(part1_out, b * QK + (i + 1))
                    nc.vector.tensor_tensor(rest[:, i % 2, :], full[:, i % 2, :], dst[:, c, 0, cols],
                                            ALU.subtract).then_inc(rest_ready, 1)
                    dve.wait_ge(rest_ready, b * QK + (i + 1))
                    nc.vector.tensor_copy(dst[:, c, 1, cols], rest[:, i % 2, :]).then_inc(part2_out, 1)
                    dve.wait_ge(part2_out, b * QK + (i + 1))
                    nc.vector.tensor_tensor(dst[:, c, 2, cols], rest[:, i % 2, :], dst[:, c, 1, cols],
                                            ALU.subtract).then_inc(split_done, 1)
                dve.wait_ge(v_stored, b * 16 + 16)
                for i in range(VG):
                    dve.wait_ge(v_projected, b * VG + (i + 1))
                    for t in range(2):
                        last = nc.vector.tensor_tensor(v_sb[:, :, 2 * i + t, 0:HD],
                                                       banks[i % 8][:, t * D:(t + 1) * D].rearrange("p (h d) -> p h d", h=H),
                                                       bv_rows[:, :].rearrange("p (h d) -> p h d", h=H), ALU.add)
                    last.then_inc(v_ready, 1)


SKEW = 3
STEPS = NT
R1 = 3 * HD + 2 * PARTS
R2 = 6 * HD + 3 * PARTS
RM = R2 - PARTS
CHUNK = 2 * N
CH = NT * (S // CHUNK)
PR = 4
XB = 3
BLOCKS = NT * NB


def attention(nc, k_parts, q_parts, v_rows, out_raw):
    with ExitStack() as ctx:
        def sb(name, shape, dt=F32):
            return ctx.enter_context(nc.sbuf_tensor("b_" + name, shape, dt))

        def sem(name):
            return ctx.enter_context(nc.semaphore("b_" + name))

        def two(make, name, *args):
            return [make(f"{name}{i}", *args) for i in range(2)]

        q1, k1 = two(sb, "q1_", [P, S], BF16), two(sb, "k1_", [P, S], BF16)
        q2, k2 = two(sb, "q2_", [P, S], BF16), two(sb, "k2_", [P, S], BF16)
        v2 = two(sb, "v_", [P, NT, VW])
        probs = sb("probs", [P, PR, S])
        chunk_max = sb("chunk_max", [P, CH])
        neg_max = sb("neg_max", [P, NT])
        neg_rest = sb("neg_rest", [P, NT])
        neg_parts = sb("neg_parts", [P, 64], BF16)
        neg_turned = two(sb, "neg_turned", [P, 64], BF16)
        out_sb = two(sb, "out_", [P, N])
        scores1 = [ctx.enter_context(nc.psum_tensor(f"b_scores1_{i}", [P, CHUNK], F32)) for i in range(2)]
        scores2 = [ctx.enter_context(nc.psum_tensor(f"b_scores2_{i}", [P, N], F32)) for i in range(XB)]
        out_ps = ctx.enter_context(nc.psum_tensor("b_out_ps", [P, N], F32))

        ones_set = sem("ones_set")
        parts_cleared = sem("parts_cleared")
        pass1_in = two(sem, "pass1_in")
        pass2_in = two(sem, "pass2_in")
        max_in = two(sem, "max_in")
        chunk_made = sem("chunk_made")
        chunk_read = sem("chunk_read")
        max_step = sem("max_step")
        max_ready = sem("max_ready")
        block_made = sem("block_made")
        exp_done = sem("exp_done")
        probs_used = sem("probs_used")
        out_copied = sem("out_copied")
        out_stored = two(sem, "out_stored")

        LOADS1, LOADS2, LOADSM = 12, 7, 8
        MS = 5

        block = ctx.enter_context(nc.Block())

        def landed(base, k, loads):
            if isinstance(base, int):
                return ((base + k) // 2 + 1) * 16 * loads
            return base * (8 * loads) + ((k + 1) // 2 * 2 + 1) * (8 * loads)

        @block.sync
        def _(sp):
            def of_head(parts, head):
                return parts[bass.ds(head, 1), :, :].rearrange("a r s -> (a r) s")

            def load_pass1(head, par):
                q, k, done = of_head(q_parts, head), of_head(k_parts, head), pass1_in[par]
                for a in (0, 64):
                    sp.dma_start(q1[par][a:a + 2 * HD, :], q[0:HD, :].partition_broadcast(2)).then_inc(done, 16)
                    sp.dma_start(q1[par][a + 2 * HD:a + 3 * HD, :], q[HD:2 * HD, :]).then_inc(done, 16)
                    sp.dma_start(q1[par][a + 3 * HD + PARTS:a + R1, :], q[3 * HD:SPLIT_ROWS, :]).then_inc(done, 16)
                    sp.dma_start(k1[par][a:a + 2 * HD, :], k[0:2 * HD, :]).then_inc(done, 16)
                    sp.dma_start(k1[par][a + 2 * HD:a + 3 * HD, :], k[0:HD, :]).then_inc(done, 16)
                    sp.dma_start(k1[par][a + 3 * HD:a + 3 * HD + PARTS, :], k[3 * HD:SPLIT_ROWS, :]).then_inc(done, 16)

            def load_pass2(head, par):
                q, k, done = of_head(q_parts, head), of_head(k_parts, head), pass2_in[par]
                two_at, one_at = SPLIT_ROWS, SPLIT_ROWS + 2 * HD
                sp.dma_start(q2[par][0:3 * HD, :], q[0:HD, :].partition_broadcast(3)).then_inc(done, 16)
                sp.dma_start(q2[par][two_at:one_at, :], q[HD:2 * HD, :].partition_broadcast(2)).then_inc(done, 16)
                sp.dma_start(q2[par][one_at:RM, :], q[2 * HD:SPLIT_ROWS, :]).then_inc(done, 16)
                sp.dma_start(k2[par][0:SPLIT_ROWS, :], k).then_inc(done, 16)
                sp.dma_start(k2[par][two_at:one_at, :], k[0:2 * HD, :]).then_inc(done, 16)
                sp.dma_start(k2[par][one_at:one_at + HD, :], k[0:HD, :]).then_inc(done, 16)
                sp.dma_start(v2[par][:, :, :].rearrange("p t w -> p (t w)"),
                             v_rows[bass.ds(head, 1), :, :].rearrange("a p n -> (a p) n")).then_inc(done, 16)

            def load_max(par):
                rows = q2[par][RM:RM + PARTS, :].rearrange("j (t a r) -> j t a r", a=4, r=32)
                for a in range(4):
                    sp.dma_start(rows[0:2, :, a, :], neg_turned[par][32 * a:32 * a + 32, 0:32]).then_inc(max_in[par], 16)
                    sp.dma_start(rows[2:3, :, a, :], neg_turned[par][32 * a:32 * a + NT, 32:64]).then_inc(max_in[par], 16)

            def period(base, k, ahead=2):
                head, par = base + k, (base + k) % 2 if isinstance(base, int) else (k + 1) % 2
                if ahead >= 2:
                    sp.wait_ge(chunk_made, (head + 1) * CH)
                    load_pass1(head + 2, par)
                if ahead >= 1:
                    sp.wait_ge(probs_used, head * NT + PR)
                    load_pass2(head + 1, 1 - par)
                    sp.wait_ge(max_ready, head + 2)
                    load_max(1 - par)
                sp.wait_ge(out_copied, head + 1)
                sp.dma_start(out_raw[bass.ds(head, 1), :, :].rearrange("a p n -> (a p) n"),
                             out_sb[par][:, :]).then_inc(out_stored[par], 16)

            sp.wait_ge(ones_set, 8)
            load_pass1(0, 0)
            load_pass1(1, 1)
            load_pass2(0, 0)
            sp.wait_ge(max_ready, 1)
            load_max(0)
            period(0, 0)
            with sp.Fori(1, BH - 3, 2) as base:
                period(base, 0)
                period(base, 1)
            period(BH - 3, 0)
            period(BH - 2, 0, ahead=1)
            period(BH - 1, 0, ahead=0)
            for par in range(2):
                sp.wait_ge(out_stored[par], 16 * (BH // 2) + 16)

        @block.tensor
        def _(pe):
            def pass1_chunk(base, k, par, c):
                t, keys = c // 2, c % 2 * CHUNK
                if c == 0:
                    pe.wait_ge(pass1_in[par], landed(base, k, LOADS1))
                pe.wait_ge(chunk_read, (base + k) * CH + (c + 1))
                for i, a in enumerate((0, 64)):
                    last = nc.tensor.matmul(scores1[c % 2][:, i * N:(i + 1) * N], q1[par][a:a + R1, t * P:(t + 1) * P],
                                            k1[par][a:a + R1, keys + i * N:keys + (i + 1) * N], start=True, stop=True)
                last.then_inc(chunk_made, 1)

            def pass2_block(base, k, par, t, j):
                b = t * NB + j
                if b == 0:
                    pe.wait_ge(pass2_in[par], landed(base, k, LOADS2))
                    pe.wait_ge(max_in[par], landed(base, k, LOADSM))
                before = b - XB if b >= XB else (-1, -3, -2)[b]
                pe.wait_ge(exp_done, (base + k) * BLOCKS + (before + 1 + XB))
                nc.tensor.matmul(scores2[b % XB][:, :], k2[par][0:R2, t * P:(t + 1) * P],
                                 q2[par][0:R2, j * N:(j + 1) * N], start=True, stop=True).then_inc(block_made, 1)

            def values(base, k, par, t):
                pe.wait_ge(exp_done, (base + k) * BLOCKS + ((t + 1) * NB + XB))
                if t == 0 and not (isinstance(base, int) and base + k == 0):
                    pe.wait_ge(out_copied, base + k)
                for j in range(NB):
                    last = nc.tensor.matmul(out_ps[32 * j:32 * j + VW, :], v2[par][:, t, :],
                                            probs[:, t % PR, j * N:(j + 1) * N], start=(t == 0), stop=(t == NT - 1))
                last.then_inc(probs_used, 1)

            def period(base, k, ahead=2):
                par = (base + k) % 2 if isinstance(base, int) else (k + 1) % 2

                def ahead_chunk(c):
                    beyond, c = divmod(c + 2 * SKEW, CH)
                    if 1 + beyond <= ahead:
                        pass1_chunk(base, k + 1 + beyond, (par + 1 + beyond) % 2, c)

                for t in range(NT):
                    ahead_chunk(2 * t)
                    pass2_block(base, k, par, t, 0)
                    pass2_block(base, k, par, t, 1)
                    if t > 0:
                        values(base, k, par, t - 1)
                    elif not (isinstance(base, int) and base + k == 0):
                        values(base, k - 1, 1 - par, NT - 1)
                    ahead_chunk(2 * t + 1)
                    pass2_block(base, k, par, t, 2)
                    pass2_block(base, k, par, t, 3)

            pe.sem_inc(probs_used, PR)
            for c in range(CH):
                pass1_chunk(0, 0, 0, c)
            for c in range(2 * SKEW):
                pass1_chunk(0, 1, 1, c)
            period(0, 0)
            with pe.Fori(1, BH - 3, 2) as base:
                period(base, 0)
                period(base, 1)
            period(BH - 3, 0)
            period(BH - 2, 0, ahead=1)
            period(BH - 1, 0, ahead=0)
            values(BH - 1, 0, 1, NT - 1)

        @block.scalar
        def _(act):
            def copy_out(base, k):
                par = (base + k) % 2 if isinstance(base, int) else (k + 1) % 2
                act.wait_ge(probs_used, (base + k + 1) * NT + PR)
                act.wait_ge(out_stored[par], landed(base, k, 1))
                nc.scalar.copy(out_sb[par][:, :], out_ps[:, :]).then_inc(out_copied, 1)

            def head(base, k):
                for t in range(NT):
                    act.wait_ge(probs_used, (base + k) * NT + (t + 1))
                    for j in range(NB):
                        b = t * NB + j
                        act.wait_ge(block_made, (base + k) * BLOCKS + (b + 1))
                        nc.scalar.activation(probs[:, t % PR, j * N:(j + 1) * N], scores2[b % XB][:, :],
                                             ACT.Exp).then_inc(exp_done, 1)
                    if t == 0 and not (isinstance(base, int) and base + k == 0):
                        copy_out(base, k - 1)

            act.sem_inc(exp_done, XB)
            for par in range(2):
                act.sem_inc(out_stored[par], 16)
            head(0, 0)
            with act.Fori(1, BH - 1, 2) as base:
                head(base, 0)
                head(base, 1)
            head(BH - 1, 0)
            copy_out(BH - 1, 0)

        @block.vector
        def _(dve):
            def head(base, k):
                first = isinstance(base, int) and base + k == 0
                par = (base + k) % 2 if isinstance(base, int) else (k + 1) % 2
                for c in range(CH):
                    dve.wait_ge(chunk_made, (base + k) * CH + (c + 1))
                    nc.vector.tensor_reduce(chunk_max[:, c:c + 1], scores1[c % 2][:, :], AX.X, ALU.max).then_inc(chunk_read, 1)
                step = [0]

                def then_next(instruction):
                    step[0] += 1
                    instruction.then_inc(max_step, 1)
                    dve.wait_ge(max_step, (base + k) * MS + step[0])

                dve.wait_ge(chunk_read, (base + k + 1) * CH + 2)
                then_next(nc.vector.tensor_reduce(neg_max[:, :], chunk_max[:, :].rearrange("p (t c) -> p t c", c=2),
                                                  AX.X, ALU.max, negate=True))
                then_next(nc.vector.tensor_copy(neg_parts[:, 0:NT], neg_max[:, :]))
                then_next(nc.vector.tensor_tensor(neg_rest[:, :], neg_max[:, :], neg_parts[:, 0:NT], ALU.subtract))
                then_next(nc.vector.tensor_copy(neg_parts[:, NT:2 * NT], neg_rest[:, :]))
                then_next(nc.vector.tensor_tensor(neg_parts[:, 2 * NT:3 * NT], neg_rest[:, :], neg_parts[:, NT:2 * NT], ALU.subtract))
                if not first:
                    dve.wait_ge(probs_used, (base + k - 1) * NT + PR)
                nc.vector.transpose(neg_turned[par][:, :], neg_parts[:, :]).then_inc(max_ready, 1)

            dve.sem_inc(chunk_read, 2)
            for operand in (*q1, *k1, *q2, *k2):
                nc.vector.memset(operand[:, :], 1.0).then_inc(ones_set, 1)
            nc.vector.memset(neg_parts[:, :], 0.0).then_inc(parts_cleared, 1)
            dve.wait_ge(parts_cleared, 1)
            head(0, 0)
            with dve.Fori(1, BH - 1, 2) as base:
                head(base, 0)
                head(base, 1)
            head(BH - 1, 0)


FB = FF // P
RT = N // P


def project_and_feed_forward(nc, x, out_raw, recips, wo, bo, u1, v1, b1, u2, v2, b2, identity_in, out):
    with ExitStack() as ctx:
        def sb(name, shape, dt=F32):
            return ctx.enter_context(nc.sbuf_tensor("c_" + name, shape, dt))

        def sem(name):
            return ctx.enter_context(nc.semaphore("c_" + name))

        def ps(name, shape):
            return ctx.enter_context(nc.psum_tensor("c_" + name, shape, F32))

        def two(make, name, *args):
            return [make(f"{name}{i}", *args) for i in range(2)]

        ident = sb("ident", [P, P])
        wo_sb = sb("wo", [P, KC, D])
        u1_sb = sb("u1", [P, KC, RANK])
        v1_sb = sb("v1", [RANK, FF])
        u2_sb = sb("u2", [P, FB, RANK])
        v2_sb = sb("v2", [RANK, D])
        b1_col = sb("b1_col", [P, FB])
        bo_rows, b2_rows = sb("bo_rows", [P, RT, D]), sb("b2_rows", [P, RT, D])
        eps = sb("eps", [P, RT])
        minus_half = sb("minus_half", [P, RT])
        sums = sb("sums", [P, 2, N])
        recip = sb("recip", [P, 2, N])
        raw, rcp = two(sb, "raw", [P, KC, N]), two(sb, "rcp", [P, KC, N])
        attn = two(sb, "attn", [P, KC, N])
        x_sb = two(sb, "x", [P, RT, D])
        y_sb = two(sb, "y", [P, RT, D])
        y_b2 = two(sb, "y_b2", [P, RT, D])
        res = sb("res", [P, RT, D])
        o_sb = two(sb, "o", [P, RT, D])
        stats = two(sb, "stats", [P, RT, 6])
        mean_var = two(sb, "mean_var", [P, RT, 2])
        var_eps = two(sb, "var_eps", [P, RT])
        rstd = two(sb, "rstd", [P, RT])
        yT = sb("yT", [P, KC, N])
        low1 = sb("low1", [RANK, N])
        hT = sb("hT", [P, FB, N])
        low2 = sb("low2", [RANK, N])
        rows_ps = ps("rows_ps", [P, RT * D])
        yT_ps = ps("yT_ps", [P, KC * N])
        low1_ps, low2_ps = ps("low1_ps", [P, N]), ps("low2_ps", [P, N])
        h_ps = two(ps, "h_ps", [P, N])

        constants_in = sem("constants_in")
        const_set = sem("const_set")
        sums_in = sem("sums_in")
        recip_made = sem("recip_made")
        recip_stored = sem("recip_stored")
        block_in = two(sem, "block_in")
        bo_added = sem("bo_added")
        divided = sem("divided")
        projected = sem("projected")
        x_added = sem("x_added")
        stat_made = two(sem, "stat_made")
        stat_seen = sem("stat_seen")
        var_made = two(sem, "var_made")
        eps_added = two(sem, "eps_added")
        rstd_made = two(sem, "rstd_made")
        y_made = sem("y_made")
        b2_added = sem("b2_added")
        turned = sem("turned")
        yT_copied = sem("yT_copied")
        low1_made = sem("low1_made")
        low1_copied = sem("low1_copied")
        h_made = sem("h_made")
        gelu_done = sem("gelu_done")
        low2_made = sem("low2_made")
        low2_copied = sem("low2_copied")
        ffn_made = sem("ffn_made")
        res_made = sem("res_made")
        o_seen = sem("o_seen")
        o_made = sem("o_made")
        stored = two(sem, "stored")

        CONSTANTS, LOADS = 9, 5

        block = ctx.enter_context(nc.Block())

        def count(b, j, per=1, start=0):
            return b * (NB * per) + ((j + 1) * per + start)

        def parity_count(b, j, per):
            return b * (NB // 2 * per) + (j // 2 + 1) * per

        def run_blocks(eng, period):
            with eng.Fori(0, B - 1) as b:
                for j in range(NB):
                    period(b, j, 2)
            for j in range(NB):
                period(B - 1, j, NB - 1 - j)

        @block.sync
        def _(sp):
            def load(b, j):
                b, j, done = b + j // NB, j % NB, block_in[j % 2]
                for c in range(KC):
                    heads = out_raw[bass.ds(b * H + c * HH, HH), :, :]
                    sp.dma_start(raw[j % 2][:, c, :], heads[:, 32 * j:32 * j + HD, :]).then_inc(done, 16)
                    sp.dma_start(rcp[j % 2][:, c, :], recips[bass.ds(b * H + c * HH, HH), j:j + 1, :]
                                 .to_broadcast([HH, HD, N])).then_inc(done, 16)
                sp.dma_start(x_sb[j % 2][:, :, :], x[bass.ds(b, 1), j * N:(j + 1) * N, :]
                             .rearrange("a (t p) d -> p (a t) d", p=P)).then_inc(done, 16)

            sp.dma_start(sums[:, :, :], out_raw.rearrange("h (j r) n -> (h j) r n", r=32)[:, HD, :]
                         .rearrange("(p l) n -> p l n", l=2)).then_inc(sums_in, 16)
            sp.dma_start(ident[:, :], identity_in).then_inc(constants_in, 16)
            sp.dma_start(wo_sb[:, :, :], wo.rearrange("(c p) n -> p c n", p=P)).then_inc(constants_in, 16)
            sp.dma_start(u1_sb[:, :, :], u1.rearrange("(c p) n -> p c n", p=P)).then_inc(constants_in, 16)
            sp.dma_start(v1_sb[:, :], v1).then_inc(constants_in, 16)
            sp.dma_start(u2_sb[:, :, :], u2.rearrange("(f p) n -> p f n", p=P)).then_inc(constants_in, 16)
            sp.dma_start(v2_sb[:, :], v2).then_inc(constants_in, 16)
            sp.dma_start(b1_col[:, :], b1.rearrange("(f p) -> p f", p=P), allow_slow_non_contiguous=True).then_inc(constants_in, 16)
            for rows, src in ((bo_rows, bo), (b2_rows, b2)):
                sp.dma_start(rows[:, :, :], src.partition_broadcast(RT).partition_broadcast(P)).then_inc(constants_in, 16)
            sp.wait_ge(recip_made, 1)
            sp.dma_start(recips.rearrange("h j n -> (h j) n").rearrange("(p l) n -> p l n", l=2),
                         recip[:, :, :]).then_inc(recip_stored, 16)
            sp.wait_ge(recip_stored, 16)
            load(0, 0)
            load(0, 1)

            def period(b, j, ahead):
                if ahead >= 2:
                    sp.wait_ge(y_made, count(b, j))
                    load(b, j + 2)
                sp.wait_ge(o_made, count(b, j))
                sp.sem_inc(o_seen, 1)
                sp.dma_start(out[bass.ds(b, 1), j * N:(j + 1) * N, :].rearrange("a (t p) d -> p (a t) d", p=P),
                             o_sb[j % 2][:, :, :]).then_inc(stored[j % 2], 16)

            run_blocks(sp, period)
            for par in range(2):
                sp.wait_ge(stored[par], 16 * (B * NB // 2) + 16)

        @block.tensor
        def _(pe):
            def project(b, j):
                pe.wait_ge(divided, count(b, j))
                pe.wait_ge(res_made, count(b, j - 2, start=2))
                for t in range(RT):
                    for c in range(KC):
                        last = nc.tensor.matmul(rows_ps[:, t * D:(t + 1) * D], attn[j % 2][:, c, t * P:(t + 1) * P],
                                                wo_sb[:, c, :], start=(c == 0), stop=(c == KC - 1))
                last.then_inc(projected, 1)

            def period(b, j, ahead):
                pe.wait_ge(y_made, count(b, j))
                pe.wait_ge(yT_copied, count(b, j - 1, start=1))
                for c in range(KC):
                    for t in range(RT):
                        last = nc.tensor.transpose(yT_ps[:, c * N + t * P:c * N + (t + 1) * P],
                                                   y_sb[j % 2][:, t, c * P:(c + 1) * P], ident[:, :])
                last.then_inc(turned, 1)
                if ahead >= 1:
                    project(b, j + 1)
                pe.wait_ge(yT_copied, count(b, j, start=1))
                pe.wait_ge(low1_copied, count(b, j - 1, start=1))
                for c in range(KC):
                    last = nc.tensor.matmul(low1_ps[0:RANK, :], u1_sb[:, c, :], yT[:, c, :],
                                            start=(c == 0), stop=(c == KC - 1))
                last.then_inc(low1_made, 1)
                pe.wait_ge(low1_copied, count(b, j, start=1))
                for f in range(FB):
                    pe.wait_ge(gelu_done, count(b, j - 1, FB, start=2) + (f - 1))
                    nc.tensor.matmul(h_ps[f % 2][:, :], v1_sb[:, f * P:(f + 1) * P], low1[:, :],
                                     start=True, stop=True).then_inc(h_made, 1)
                pe.wait_ge(low2_copied, count(b, j - 1, start=1))
                for f in range(FB):
                    pe.wait_ge(gelu_done, count(b, j - 1, FB, start=2) + (f + 1))
                    last = nc.tensor.matmul(low2_ps[0:RANK, :], u2_sb[:, f, :], hT[:, f, :],
                                            start=(f == 0), stop=(f == FB - 1))
                last.then_inc(low2_made, 1)
                pe.wait_ge(low2_copied, count(b, j, start=1))
                if ahead >= 1:
                    pe.wait_ge(x_added, count(b, j + 1, start=1))
                else:
                    pe.wait_ge(res_made, count(b, j - 1, start=2))
                for t in range(RT):
                    last = nc.tensor.matmul(rows_ps[:, t * D:(t + 1) * D], low2[:, t * P:(t + 1) * P], v2_sb[:, :],
                                            start=True, stop=True)
                last.then_inc(ffn_made, 1)

            pe.sem_inc(turned, 1)
            pe.sem_inc(low1_made, 1)
            pe.sem_inc(h_made, FB)
            pe.sem_inc(low2_made, 1)
            pe.sem_inc(ffn_made, 1)
            pe.wait_ge(constants_in, 16 * CONSTANTS)
            project(0, 0)
            run_blocks(pe, period)

        @block.scalar
        def _(act):
            def period(b, j, ahead):
                act.wait_ge(turned, count(b, j, start=1))
                act.wait_ge(low1_made, count(b, j - 1, start=1))
                nc.scalar.copy(yT[:, :, :].rearrange("p c n -> p (c n)"), yT_ps[:, :]).then_inc(yT_copied, 1)
                act.wait_ge(low1_made, count(b, j, start=1))
                act.wait_ge(h_made, count(b, j - 1, FB, start=FB))
                nc.scalar.copy(low1[:, :], low1_ps[0:RANK, :]).then_inc(low1_copied, 1)
                act.wait_ge(low2_made, count(b, j - 1, start=1))
                for f in range(FB):
                    act.wait_ge(h_made, count(b, j - 1, FB, start=FB) + (f + 1))
                    nc.scalar.activation(hT[:, f, :], h_ps[f % 2][:, :], ACT.Gelu_apprx_tanh,
                                         bias=b1_col[:, f:f + 1]).then_inc(gelu_done, 1)
                act.wait_ge(low2_made, count(b, j, start=1))
                act.wait_ge(ffn_made, count(b, j - 1, start=1))
                nc.scalar.copy(low2[:, :], low2_ps[0:RANK, :]).then_inc(low2_copied, 1)

            act.sem_inc(yT_copied, 1)
            act.sem_inc(low1_copied, 1)
            act.sem_inc(gelu_done, 2)
            act.sem_inc(low2_copied, 1)
            act.wait_ge(constants_in, 16 * CONSTANTS)
            run_blocks(act, period)

        @block.vector
        def _(dve):
            def divide(b, j):
                dve.wait_ge(block_in[j % 2], parity_count(b, j, 16 * LOADS))
                if not (isinstance(b, int) and b == 0 and j < 2):
                    dve.wait_ge(projected, count(b, j - 2))
                nc.vector.tensor_tensor(attn[j % 2][:, :, :], raw[j % 2][:, :, :], rcp[j % 2][:, :, :],
                                        ALU.mult).then_inc(divided, 1)

            def norm(which, src, dst, b, j, done):
                for t in range(RT):
                    nc.vector.bn_stats(stats[which][:, t, :], src[:, t, :]).then_inc(stat_made[which], 1)
                dve.wait_ge(stat_made[which], count(b, j, RT))
                dve.sem_inc(stat_seen, 1)
                for t in range(RT):
                    last = nc.vector.bn_aggr(mean_var[which][:, t, :], stats[which][:, t, :])
                last.then_inc(var_made[which], 1)
                dve.wait_ge(rstd_made[which], count(b, j))
                dve.wait_ge(var_made[which], count(b, j))
                for t in range(RT):
                    last = nc.vector.tensor_scalar(dst[:, t, :], src[:, t, :], mean_var[which][:, t, 0:1],
                                                   rstd[which][:, t:t + 1], ALU.subtract, ALU.mult)
                last.then_inc(done, 1)

            def first_norm(b, j):
                dve.wait_ge(bo_added, count(b, j))
                dve.wait_ge(projected, count(b, j))
                rows = x_sb[j % 2][:, :, :].rearrange("p t d -> p (t d)")
                nc.vector.tensor_tensor(rows, rows_ps[:, :], rows, ALU.add).then_inc(x_added, 1)
                dve.wait_ge(x_added, count(b, j, start=1))
                norm(0, x_sb[j % 2], y_sb[j % 2], b, j, y_made)

            def period(b, j, ahead):
                if ahead >= 1:
                    first_norm(b, j + 1)
                else:
                    dve.wait_ge(o_made, count(b, j - 1))
                dve.wait_ge(b2_added, count(b, j))
                dve.wait_ge(ffn_made, count(b, j, start=1))
                nc.vector.tensor_tensor(res[:, :, :].rearrange("p t d -> p (t d)"), rows_ps[:, :],
                                        y_b2[j % 2][:, :, :].rearrange("p t d -> p (t d)"), ALU.add).then_inc(res_made, 1)
                dve.wait_ge(res_made, count(b, j, start=2))
                dve.wait_ge(stored[j % 2], parity_count(b, j, 16))
                norm(1, res, o_sb[j % 2], b, j, o_made)
                if ahead >= 2:
                    divide(b, j + 2)

            dve.sem_inc(x_added, 1)
            dve.sem_inc(res_made, 2)
            for par in range(2):
                dve.sem_inc(stored[par], 16)
            nc.vector.memset(minus_half[:, :], -0.5).then_inc(const_set, 1)
            nc.vector.memset(eps[:, :], EPS).then_inc(const_set, 1)
            dve.wait_ge(sums_in, 16)
            nc.vector.reciprocal(recip[:, :, :], sums[:, :, :]).then_inc(recip_made, 1)
            divide(0, 0)
            divide(0, 1)
            first_norm(0, 0)
            run_blocks(dve, period)

        @block.gpsimd
        def _(pool):
            def rstd_of(which, b, j):
                pool.wait_ge(var_made[which], count(b, j))
                nc.gpsimd.tensor_tensor(var_eps[which][:, :], mean_var[which][:, :, 1], eps[:, :],
                                        ALU.add).then_inc(eps_added[which], 1)
                pool.wait_ge(eps_added[which], count(b, j))
                nc.gpsimd.tensor_tensor(rstd[which][:, :], var_eps[which][:, :], minus_half[:, :],
                                        ALU.pow).then_inc(rstd_made[which], 1)

            def add_bo(b, j):
                pool.wait_ge(block_in[j % 2], parity_count(b, j, 16 * LOADS))
                nc.gpsimd.tensor_tensor(x_sb[j % 2][:, :, :], x_sb[j % 2][:, :, :], bo_rows[:, :, :],
                                        ALU.add).then_inc(bo_added, 1)

            def after_first_norm(b, j):
                rstd_of(0, b, j)
                pool.wait_ge(y_made, count(b, j))
                if not (isinstance(b, int) and b == 0 and j < 2):
                    pool.wait_ge(res_made, count(b, j - 2, start=2))
                nc.gpsimd.tensor_tensor(y_b2[j % 2][:, :, :], y_sb[j % 2][:, :, :], b2_rows[:, :, :],
                                        ALU.add).then_inc(b2_added, 1)

            def period(b, j, ahead):
                if ahead >= 1:
                    after_first_norm(b, j + 1)
                rstd_of(1, b, j)
                if ahead >= 2:
                    add_bo(b, j + 2)

            pool.wait_ge(constants_in, 16 * CONSTANTS)
            pool.wait_ge(const_set, 2)
            add_bo(0, 0)
            add_bo(0, 1)
            after_first_norm(0, 0)
            run_blocks(pool, period)


def build(nc, x, wq, bq, wk, bk, wv, bv, wo, bo, u1, v1, b1, u2, v2, b2, alibi_k, alibi_q, identity, out):
    k_parts = nc.dram_tensor("k_parts", [BH, SPLIT_ROWS, S], BF16).ap()
    q_parts = nc.dram_tensor("q_parts", [BH, SPLIT_ROWS, S], BF16).ap()
    v_rows = nc.dram_tensor("v_rows", [BH, P, NT * VW], F32).ap()
    out_raw = nc.dram_tensor("out_raw", [BH, P, N], F32).ap()
    recips = nc.dram_tensor("recips", [BH, NB, N], F32).ap()
    project_and_split(nc, x, {"q": wq, "k": wk, "v": wv}, {"q": bq, "k": bk, "v": bv}, alibi_k, alibi_q,
                      k_parts, q_parts, v_rows, identity)
    attention(nc, k_parts, q_parts, v_rows, out_raw)
    project_and_feed_forward(nc, x, out_raw, recips, wo, bo, u1, v1, b1, u2, v2, b2, identity, out)


INPUTS = ["L0_attn_x", "L0_attn_Wq", "L0_attn_bq", "L0_attn_Wk", "L0_attn_bk", "L0_attn_Wv", "L0_attn_bv",
          "L0_attn_Wo", "L0_attn_bo", "L0_ffn_U1", "L0_ffn_V1", "L0_ffn_b1", "L0_ffn_U2", "L0_ffn_V2", "L0_ffn_b2"]


def kernel(**inputs):
    import concourse.bacc as bacc
    from concourse.bass_utils import run_bass_kernel_spmd

    nc = bacc.Bacc("TRN2", target_bir_lowering=False, num_devices=1)
    alibi_k, alibi_q = alibi_rows()
    arrays = {name: np.ascontiguousarray(inputs[name]) for name in INPUTS}
    arrays |= {"alibi_k": alibi_k, "alibi_q": alibi_q, "identity": np.eye(P, dtype=np.float32)}
    args = [nc.dram_tensor(name, a.shape, mybir.dt.from_np(a.dtype), kind="ExternalInput").ap()
            for name, a in arrays.items()]
    out = nc.dram_tensor("out", (B, S, D), F32, kind="ExternalOutput").ap()
    build(nc, *args, out)
    return run_bass_kernel_spmd(nc, [arrays], core_ids=[0]).results[0]["out"]
```

```python
from contextlib import ExitStack

import numpy as np

import concourse.bass as bass
from concourse import mybir

F32 = mybir.dt.float32
BF16 = mybir.dt.bfloat16
ALU = mybir.AluOpType
ACT = mybir.ActivationFunctionType
AX = mybir.AxisListType

P = 128
B, S, D = 4, 2048, 256
H = 16
HD = D // H
BH = B * H
KC = D // P
HH = H // KC
NT = S // P
N = 512
NB = S // N
FF, RANK = 1024, 64
EPS = 1e-5
SCALE = float(HD) ** -0.5
PARTS = 3
SPLIT_ROWS = PARTS * HD + PARTS
VW = 2 * HD


def split_constant(x):
    parts, rest = [], x.astype(np.float32)
    for _ in range(PARTS):
        part = rest.astype(mybir.dt.np(BF16))
        parts.append(part)
        rest = rest - part.astype(np.float32)
    return np.stack(parts, axis=-2)


def alibi_rows():
    slopes = (1.0 / 2.0 ** (np.arange(H, dtype=np.float32) / H)).astype(np.float32)
    ramp = slopes[:, None] * np.arange(S, dtype=np.float32)[None, :]
    return split_constant(ramp), split_constant(-ramp)


def project_and_split(nc, x, weights, biases, alibi_k, alibi_q, k_parts, q_parts, v_rows, identity_in):
    names = ("q", "k")
    with ExitStack() as ctx:
        def sb(name, shape, dt=F32):
            return ctx.enter_context(nc.sbuf_tensor("a_" + name, shape, dt))

        def sem(name):
            return ctx.enter_context(nc.semaphore("a_" + name))

        ident = sb("ident", [P, P])
        w_sb = {n: sb("w" + n, [P, KC, D]) for n in "qkv"}
        bias_col = {n: sb("bias_" + n, [P, KC]) for n in names}
        bq_scaled = sb("bq_scaled", [P, KC])
        bv_rows = sb("bv_rows", [P, D])
        x_sb = sb("x", [P, NT, D])
        xT = sb("xT", [P, KC, S])
        full = sb("full", [P, 2, N])
        rest = sb("rest", [P, 2, N])
        parts = {n: sb("parts_" + n, [P, KC, PARTS, S], BF16) for n in names}
        v_sb = sb("v", [P, H, NT, VW])
        banks = [ctx.enter_context(nc.psum_tensor(f"a_bank{i}", [P, N], F32)) for i in range(8)]

        constants_in = sem("constants_in")
        x_in = sem("x_in")
        bias_scaled = sem("bias_scaled")
        ones_set = sem("ones_set")
        transposed = sem("transposed")
        xT_ready = sem("xT_ready")
        projected = sem("projected")
        part1_out = sem("part1_out")
        rest_ready = sem("rest_ready")
        part2_out = sem("part2_out")
        split_seen = sem("split_seen")
        split_done = sem("split_done")
        v_projected = sem("v_projected")
        v_ready = sem("v_ready")
        parts_stored = sem("parts_stored")
        v_stored = sem("v_stored")
        alibi_stored = sem("alibi_stored")

        XG = KC * NB
        QK = 2 * KC * NB
        VG = NT // 2
        tiles = [(n, c, j) for j in range(NB) for n in range(2) for c in range(KC)]
        stores = 2 * KC * PARTS

        block = ctx.enter_context(nc.Block())

        @block.sync
        def _(sp):
            sp.dma_start(ident[:, :], identity_in).then_inc(constants_in, 16)
            for n in "qkv":
                sp.dma_start(w_sb[n][:, :, :], weights[n].rearrange("(c p) n -> p c n", p=P)).then_inc(constants_in, 16)
            for n in names:
                sp.dma_start(bias_col[n][:, :], biases[n].rearrange("(c p) -> p c", p=P),
                             allow_slow_non_contiguous=True).then_inc(constants_in, 16)
            sp.dma_start(bv_rows[:, :], biases["v"].partition_broadcast(P)).then_inc(constants_in, 16)

            def load_x(b):
                sp.dma_start(x_sb[:, :, :], x[bass.ds(b, 1), :, :].rearrange("a (t p) d -> p (a t) d", p=P)).then_inc(x_in, 16)

            def store(b, more=True):
                if more:
                    sp.wait_ge(transposed, b * XG + XG)
                    load_x(b + 1)
                for src, dst in ((alibi_q, q_parts), (alibi_k, k_parts)):
                    sp.dma_start(dst[bass.ds(b * H, H), PARTS * HD:SPLIT_ROWS, :], src).then_inc(alibi_stored, 16)
                sp.wait_ge(split_done, b * QK + QK)
                sp.sem_inc(split_seen, 1)
                for n, dst in ((0, q_parts), (1, k_parts)):
                    for c in range(KC):
                        for j in range(PARTS):
                            sp.dma_start(dst[bass.ds(b * H + c * HH, HH), j * HD:(j + 1) * HD, :],
                                         parts[names[n]][:, c, j, :]).then_inc(parts_stored, 16)
                sp.wait_ge(v_ready, b * VG + VG + 1)
                sp.dma_start(v_rows[bass.ds(b * H, H), :, :].rearrange("h p n -> p h n"),
                             v_sb[:, :, :, :].rearrange("p h t w -> p h (t w)")).then_inc(v_stored, 16)
            load_x(0)
            with sp.Fori(0, B - 1) as b:
                store(b)
            store(B - 1, more=False)
            sp.wait_ge(parts_stored, 16 * stores * B + 16)
            sp.wait_ge(v_stored, 16 * B + 16)
            sp.wait_ge(alibi_stored, 32 * B)

        @block.tensor
        def _(pe):
            pe.wait_ge(constants_in, 16 * 7)
            with pe.Fori(0, B) as b:
                pe.wait_ge(x_in, b * 16 + 16)
                g = 0
                for j in range(NB):
                    for c in range(KC):
                        pe.wait_ge(v_ready, b * VG + 1)
                        for i in range(NB):
                            last = nc.tensor.transpose(banks[g][:, i * P:(i + 1) * P],
                                                       x_sb[:, j * 4 + i, c * P:(c + 1) * P], ident[:, :])
                        last.then_inc(transposed, 1)
                        g += 1
                pe.wait_ge(xT_ready, b * XG + XG)
                for i, (n, c, j) in enumerate(tiles):
                    if i >= 8:
                        pe.wait_ge(part1_out, b * QK + i - 7)
                    for h in range(KC):
                        last = nc.tensor.matmul(banks[i % 8][:, :], w_sb[names[n]][:, h, c * P:(c + 1) * P],
                                                xT[:, h, j * N:(j + 1) * N], start=(h == 0), stop=(h == KC - 1))
                    last.then_inc(projected, 1)
                for i in range(VG):
                    pe.wait_ge(part1_out, b * QK + QK - 7 + i)
                    for t in range(2):
                        for h in range(KC):
                            last = nc.tensor.matmul(banks[i % 8][:, t * D:(t + 1) * D],
                                                    xT[:, h, (2 * i + t) * P:(2 * i + t + 1) * P], w_sb["v"][:, h, :],
                                                    start=(h == 0), stop=(h == KC - 1))
                    last.then_inc(v_projected, 1)

        @block.scalar
        def _(act):
            act.sem_inc(parts_stored, 16)
            act.wait_ge(constants_in, 16 * 7)
            nc.scalar.mul(bq_scaled[:, :], bias_col["q"][:, :], SCALE).then_inc(bias_scaled, 1)
            act.wait_ge(bias_scaled, 1)
            with act.Fori(0, B) as b:
                act.wait_ge(parts_stored, b * (16 * stores) + 16)
                for i, (n, c, j) in enumerate(tiles):
                    act.wait_ge(projected, b * QK + (i + 1))
                    if i >= 2:
                        act.wait_ge(split_done, b * QK + (i - 1))
                    bias = bq_scaled if n == 0 else bias_col["k"]
                    scale = SCALE if n == 0 else 1.0
                    nc.scalar.activation(full[:, i % 2, :], banks[i % 8][:, :], ACT.Identity,
                                         bias=bias[:, c:c + 1], scale=scale)
                    nc.scalar.activation(parts[names[n]][:, c, 0, j * N:(j + 1) * N], banks[i % 8][:, :], ACT.Identity,
                                         bias=bias[:, c:c + 1], scale=scale).then_inc(part1_out, 1)

        @block.vector
        def _(dve):
            dve.sem_inc(v_ready, 1)
            dve.sem_inc(v_stored, 16)
            nc.vector.memset(v_sb[:, :, :, :], 1.0).then_inc(ones_set, 1)
            dve.wait_ge(ones_set, 1)
            dve.wait_ge(constants_in, 16 * 7)
            with dve.Fori(0, B) as b:
                g = 0
                for j in range(NB):
                    for c in range(KC):
                        dve.wait_ge(transposed, b * XG + (g + 1))
                        nc.vector.tensor_copy(xT[:, c, j * N:(j + 1) * N], banks[g][:, :]).then_inc(xT_ready, 1)
                        g += 1
                for i, (n, c, j) in enumerate(tiles):
                    dst = parts[names[n]]
                    cols = slice(j * N, (j + 1) * N)
                    dve.wait_ge(part1_out, b * QK + (i + 1))
                    nc.vector.tensor_tensor(rest[:, i % 2, :], full[:, i % 2, :], dst[:, c, 0, cols],
                                            ALU.subtract).then_inc(rest_ready, 1)
                    dve.wait_ge(rest_ready, b * QK + (i + 1))
                    nc.vector.tensor_copy(dst[:, c, 1, cols], rest[:, i % 2, :]).then_inc(part2_out, 1)
                    dve.wait_ge(part2_out, b * QK + (i + 1))
                    nc.vector.tensor_tensor(dst[:, c, 2, cols], rest[:, i % 2, :], dst[:, c, 1, cols],
                                            ALU.subtract).then_inc(split_done, 1)
                dve.wait_ge(v_stored, b * 16 + 16)
                for i in range(VG):
                    dve.wait_ge(v_projected, b * VG + (i + 1))
                    for t in range(2):
                        last = nc.vector.tensor_tensor(v_sb[:, :, 2 * i + t, 0:HD],
                                                       banks[i % 8][:, t * D:(t + 1) * D].rearrange("p (h d) -> p h d", h=H),
                                                       bv_rows[:, :].rearrange("p (h d) -> p h d", h=H), ALU.add)
                    last.then_inc(v_ready, 1)


SKEW = 3
STEPS = NT
R1 = 3 * HD + 2 * PARTS
R2 = 6 * HD + 3 * PARTS
RM = R2 - PARTS
CHUNK = 2 * N
CH = NT * (S // CHUNK)
LAG = 2
PR = 4
XB = 3
BLOCKS = NT * NB


def attention(nc, k_parts, q_parts, v_rows, out_raw, identity_in):
    with ExitStack() as ctx:
        def sb(name, shape, dt=F32):
            return ctx.enter_context(nc.sbuf_tensor("b_" + name, shape, dt))

        def sem(name):
            return ctx.enter_context(nc.semaphore("b_" + name))

        def two(make, name, *args):
            return [make(f"{name}{i}", *args) for i in range(2)]

        q1, k1 = two(sb, "q1_", [P, S], BF16), two(sb, "k1_", [P, S], BF16)
        q2, k2 = two(sb, "q2_", [P, S], BF16), two(sb, "k2_", [P, S], BF16)
        v2 = two(sb, "v_", [P, NT, VW])
        probs = sb("probs", [P, PR, S])
        chunk_max = two(sb, "chunk_max", [P, CH])
        neg_max = two(sb, "neg_max", [P, NT])
        neg_rest = two(sb, "neg_rest", [P, NT])
        zeros = sb("zeros", [P, NT])
        neg_parts = two(sb, "neg_parts", [P, P], BF16)
        neg_rows = two(sb, "neg_rows", [PARTS * NT, P], BF16)
        ident = sb("ident", [P, P], BF16)
        out_sb = two(sb, "out_", [P, N])
        scores1 = [ctx.enter_context(nc.psum_tensor(f"b_scores1_{i}", [P, CHUNK], F32)) for i in range(2)]
        scores2 = [ctx.enter_context(nc.psum_tensor(f"b_scores2_{i}", [P, N], F32)) for i in range(XB)]
        out_ps = ctx.enter_context(nc.psum_tensor("b_out_ps", [P, N], F32))

        ones_set = sem("ones_set")
        pool_cleared = sem("pool_cleared")
        pass1_in = two(sem, "pass1_in")
        pass2_in = two(sem, "pass2_in")
        max_in = two(sem, "max_in")
        chunk_made = sem("chunk_made")
        chunk_read = sem("chunk_read")
        negated = sem("negated")
        part_split = sem("part_split")
        max_split = sem("max_split")
        max_turned = sem("max_turned")
        max_ready = sem("max_ready")
        ident_in = sem("ident_in")
        block_made = sem("block_made")
        exp_done = sem("exp_done")
        probs_used = sem("probs_used")
        out_copied = sem("out_copied")
        out_stored = two(sem, "out_stored")

        LOADS1, LOADS2, LOADSM = 12, 7, 1
        TURN_AT = 2

        block = ctx.enter_context(nc.Block())

        def landed(base, k, loads):
            if isinstance(base, int):
                return ((base + k) // 2 + 1) * 16 * loads
            return base * (8 * loads) + ((k + 1) // 2 * 2 + 1) * (8 * loads)

        @block.sync
        def _(sp):
            def of_head(parts, head):
                return parts[bass.ds(head, 1), :, :].rearrange("a r s -> (a r) s")

            def load_pass1(head, par):
                q, k, done = of_head(q_parts, head), of_head(k_parts, head), pass1_in[par]
                for a in (0, 64):
                    sp.dma_start(q1[par][a:a + 2 * HD, :], q[0:HD, :].partition_broadcast(2)).then_inc(done, 16)
                    sp.dma_start(q1[par][a + 2 * HD:a + 3 * HD, :], q[HD:2 * HD, :]).then_inc(done, 16)
                    sp.dma_start(q1[par][a + 3 * HD + PARTS:a + R1, :], q[3 * HD:SPLIT_ROWS, :]).then_inc(done, 16)
                    sp.dma_start(k1[par][a:a + 2 * HD, :], k[0:2 * HD, :]).then_inc(done, 16)
                    sp.dma_start(k1[par][a + 2 * HD:a + 3 * HD, :], k[0:HD, :]).then_inc(done, 16)
                    sp.dma_start(k1[par][a + 3 * HD:a + 3 * HD + PARTS, :], k[3 * HD:SPLIT_ROWS, :]).then_inc(done, 16)

            def load_pass2(head, par):
                q, k, done = of_head(q_parts, head), of_head(k_parts, head), pass2_in[par]
                two_at, one_at = SPLIT_ROWS, SPLIT_ROWS + 2 * HD
                sp.dma_start(q2[par][0:3 * HD, :], q[0:HD, :].partition_broadcast(3)).then_inc(done, 16)
                sp.dma_start(q2[par][two_at:one_at, :], q[HD:2 * HD, :].partition_broadcast(2)).then_inc(done, 16)
                sp.dma_start(q2[par][one_at:RM, :], q[2 * HD:SPLIT_ROWS, :]).then_inc(done, 16)
                sp.dma_start(k2[par][0:SPLIT_ROWS, :], k).then_inc(done, 16)
                sp.dma_start(k2[par][two_at:one_at, :], k[0:2 * HD, :]).then_inc(done, 16)
                sp.dma_start(k2[par][one_at:one_at + HD, :], k[0:HD, :]).then_inc(done, 16)
                sp.dma_start(v2[par][:, :, :].rearrange("p t w -> p (t w)"),
                             v_rows[bass.ds(head, 1), :, :].rearrange("a p n -> (a p) n")).then_inc(done, 16)

            def load_max(par):
                sp.dma_start(q2[par][RM:RM + PARTS, :].rearrange("j (t q) -> j t q", q=P), neg_rows[par][:, :]).then_inc(max_in[par], 16)

            def period(base, k, ahead=2):
                head, par = base + k, (base + k) % 2 if isinstance(base, int) else (k + 1) % 2
                if ahead >= 2:
                    sp.wait_ge(chunk_made, (head + 1) * CH)
                    load_pass1(head + 2, par)
                if ahead >= 1:
                    sp.wait_ge(probs_used, head * NT + PR)
                    load_pass2(head + 1, 1 - par)
                    sp.wait_ge(max_ready, head + 2)
                    load_max(1 - par)
                sp.wait_ge(out_copied, head + 1)
                sp.dma_start(out_raw[bass.ds(head, 1), :, :].rearrange("a p n -> (a p) n"),
                             out_sb[par][:, :]).then_inc(out_stored[par], 16)

            sp.dma_start(ident[:, :], identity_in).then_inc(ident_in, 16)
            sp.wait_ge(ones_set, 8)
            load_pass1(0, 0)
            load_pass1(1, 1)
            load_pass2(0, 0)
            sp.wait_ge(max_ready, 1)
            load_max(0)
            period(0, 0)
            with sp.Fori(1, BH - 3, 2) as base:
                period(base, 0)
                period(base, 1)
            period(BH - 3, 0)
            period(BH - 2, 0, ahead=1)
            period(BH - 1, 0, ahead=0)
            for par in range(2):
                sp.wait_ge(out_stored[par], 16 * (BH // 2) + 16)

        @block.tensor
        def _(pe):
            def pass1_chunk(base, k, par, c):
                t, keys = c // 2, c % 2 * CHUNK
                if c == 0:
                    pe.wait_ge(pass1_in[par], landed(base, k, LOADS1))
                if c == TURN_AT + 1 and not (isinstance(base, int) and base + k == 0):
                    pe.wait_ge(max_ready, base + k)
                pe.wait_ge(chunk_read, (base + k) * CH + (c + 1))
                for i, a in enumerate((0, 64)):
                    last = nc.tensor.matmul(scores1[c % 2][:, i * N:(i + 1) * N], q1[par][a:a + R1, t * P:(t + 1) * P],
                                            k1[par][a:a + R1, keys + i * N:keys + (i + 1) * N], start=True, stop=True)
                last.then_inc(chunk_made, 1)

            def turn_max(base, k, par):
                pe.wait_ge(max_split, base + k + 1)
                last = isinstance(base, int) and base + k == BH - 1
                pe.wait_ge(chunk_read, (base + k + 1) * CH + (2 if last else TURN_AT + 2))
                nc.tensor.transpose(scores1[(TURN_AT + 1) % 2][:, :].bitcast(BF16)[:, 0:P],
                                    neg_parts[par][:, :], ident[:, :]).then_inc(max_turned, 1)

            def pass2_block(base, k, par, t, j):
                b = t * NB + j
                if b == 0:
                    pe.wait_ge(pass2_in[par], landed(base, k, LOADS2))
                    pe.wait_ge(max_in[par], landed(base, k, LOADSM))
                before = b - XB if b >= XB else ((-2, -1, -3), (-3, -2, -1))[par][b]
                pe.wait_ge(exp_done, (base + k) * BLOCKS + (before + 1 + XB))
                nc.tensor.matmul(scores2[(b + par) % XB][:, :], k2[par][0:R2, t * P:(t + 1) * P],
                                 q2[par][0:R2, j * N:(j + 1) * N], start=True, stop=True).then_inc(block_made, 1)

            def values(base, k, par, t):
                pe.wait_ge(exp_done, (base + k) * BLOCKS + ((t + 1) * NB + XB))
                if t == 0 and not (isinstance(base, int) and base + k == 0):
                    pe.wait_ge(out_copied, base + k)
                for j in range(NB):
                    last = nc.tensor.matmul(out_ps[32 * j:32 * j + VW, :], v2[par][:, t, :],
                                            probs[:, t % PR, j * N:(j + 1) * N], start=(t == 0), stop=(t == NT - 1))
                last.then_inc(probs_used, 1)

            def period(base, k, ahead=2):
                par = (base + k) % 2 if isinstance(base, int) else (k + 1) % 2

                def ahead_chunk(c):
                    beyond, c = divmod(c + 2 * SKEW, CH)
                    if 1 + beyond <= ahead:
                        pass1_chunk(base, k + 1 + beyond, (par + 1 + beyond) % 2, c)

                for t in range(NT):
                    ahead_chunk(2 * t)
                    pass2_block(base, k, par, t, 0)
                    pass2_block(base, k, par, t, 1)
                    if 2 * (t + SKEW) == CH + TURN_AT and ahead >= 1:
                        turn_max(base, k + 1, 1 - par)
                    if t >= LAG:
                        values(base, k, par, t - LAG)
                    elif not (isinstance(base, int) and base + k == 0):
                        values(base, k - 1, 1 - par, NT + t - LAG)
                    ahead_chunk(2 * t + 1)
                    pass2_block(base, k, par, t, 2)
                    pass2_block(base, k, par, t, 3)

            pe.sem_inc(probs_used, PR)
            for c in range(CH):
                pass1_chunk(0, 0, 0, c)
            pe.wait_ge(ident_in, 16)
            for c in range(2 * SKEW):
                pass1_chunk(0, 1, 1, c)
                if c == TURN_AT:
                    turn_max(0, 0, 0)
            period(0, 0)
            with pe.Fori(1, BH - 3, 2) as base:
                period(base, 0)
                period(base, 1)
            period(BH - 3, 0)
            period(BH - 2, 0, ahead=1)
            period(BH - 1, 0, ahead=0)
            for t in range(NT - LAG, NT):
                values(BH - 1, 0, 1, t)

        @block.scalar
        def _(act):
            def copy_out(base, k):
                par = (base + k) % 2 if isinstance(base, int) else (k + 1) % 2
                act.wait_ge(probs_used, (base + k + 1) * NT + PR)
                act.wait_ge(out_stored[par], landed(base, k, 1))
                nc.scalar.copy(out_sb[par][:, :], out_ps[:, :]).then_inc(out_copied, 1)

            def copy_max(base, k, par):
                act.wait_ge(max_turned, base + k + 1)
                nc.scalar.copy(neg_rows[par][:, :], scores1[(TURN_AT + 1) % 2][:, :].bitcast(BF16)[0:PARTS * NT, 0:P]).then_inc(max_ready, 1)

            def head(base, k, last=False):
                par = (base + k) % 2 if isinstance(base, int) else (k + 1) % 2
                for t in range(NT):
                    act.wait_ge(probs_used, (base + k) * NT + (t + 1))
                    for j in range(NB):
                        b = t * NB + j
                        act.wait_ge(block_made, (base + k) * BLOCKS + (b + 1))
                        nc.scalar.activation(probs[:, t % PR, j * N:(j + 1) * N], scores2[(b + par) % XB][:, :],
                                             ACT.Exp).then_inc(exp_done, 1)
                        if b == LAG * NB - 2 and not (isinstance(base, int) and base + k == 0):
                            copy_out(base, k - 1)
                        if 2 * (t + SKEW) == CH + TURN_AT and j == 1 and not last:
                            copy_max(base, k + 1, 1 - par)

            act.sem_inc(exp_done, XB)
            for par in range(2):
                act.sem_inc(out_stored[par], 16)
            copy_max(0, 0, 0)
            head(0, 0)
            with act.Fori(1, BH - 1, 2) as base:
                head(base, 0)
                head(base, 1)
            head(BH - 1, 0, last=True)
            copy_out(BH - 1, 0)

        @block.vector
        def _(dve):
            def parity(base, k):
                return (base + k) % 2 if isinstance(base, int) else (k + 1) % 2

            def negate(base, k):
                par = parity(base, k)
                dve.wait_ge(chunk_read, (base + k + 1) * CH + 2)
                nc.vector.tensor_reduce(neg_max[par][:, :], chunk_max[par][:, :].rearrange("p (t c) -> p t c", c=2),
                                        AX.X, ALU.max, negate=True).then_inc(negated, 1)

            def head(base, k):
                par = parity(base, k)
                for c in range(CH):
                    dve.wait_ge(chunk_made, (base + k) * CH + (c + 1))
                    nc.vector.tensor_reduce(chunk_max[par][:, c:c + 1], scores1[c % 2][:, :], AX.X, ALU.max).then_inc(chunk_read, 1)
                negate(base, k)

            dve.sem_inc(chunk_read, 2)
            for operand in (*q1, *k1, *q2, *k2):
                nc.vector.memset(operand[:, :], 1.0).then_inc(ones_set, 1)
            head(0, 0)
            with dve.Fori(1, BH - 1, 2) as base:
                head(base, 0)
                head(base, 1)
            head(BH - 1, 0)

        @block.gpsimd
        def _(pool):
            def split(base, k):
                par = (base + k) % 2 if isinstance(base, int) else (k + 1) % 2
                whole, rest, parts = neg_max[par], neg_rest[par], neg_parts[par]
                pool.wait_ge(negated, base + k + 1)
                nc.gpsimd.tensor_tensor(parts[:, 0:NT], whole[:, :], zeros[:, :], ALU.add).then_inc(part_split, 1)
                pool.wait_ge(part_split, (base + k) * 3 + 1)
                nc.gpsimd.tensor_tensor(rest[:, :], whole[:, :], parts[:, 0:NT], ALU.subtract).then_inc(part_split, 1)
                pool.wait_ge(part_split, (base + k) * 3 + 2)
                nc.gpsimd.tensor_tensor(parts[:, NT:2 * NT], rest[:, :], zeros[:, :], ALU.add).then_inc(part_split, 1)
                pool.wait_ge(part_split, (base + k) * 3 + 3)
                nc.gpsimd.tensor_tensor(parts[:, 2 * NT:3 * NT], rest[:, :], parts[:, NT:2 * NT], ALU.subtract).then_inc(max_split, 1)

            nc.gpsimd.memset(zeros[:, :], 0.0).then_inc(pool_cleared, 1)
            for par in range(2):
                nc.gpsimd.memset(neg_parts[par][:, :], 0.0).then_inc(pool_cleared, 1)
            pool.wait_ge(pool_cleared, 3)
            split(0, 0)
            with pool.Fori(1, BH - 1, 2) as base:
                split(base, 0)
                split(base, 1)
            split(BH - 1, 0)


FB = FF // P
RT = N // P
HN = N // 2


def project_and_feed_forward(nc, x, out_raw, recips, wo, bo, u1, v1, b1, u2, v2, b2, identity_in, out):
    with ExitStack() as ctx:
        def sb(name, shape, dt=F32):
            return ctx.enter_context(nc.sbuf_tensor("c_" + name, shape, dt))

        def sem(name):
            return ctx.enter_context(nc.semaphore("c_" + name))

        def ps(name, shape):
            return ctx.enter_context(nc.psum_tensor("c_" + name, shape, F32))

        def two(make, name, *args):
            return [make(f"{name}{i}", *args) for i in range(2)]

        ident = sb("ident", [P, P])
        wo_sb = sb("wo", [P, KC, D])
        u1_sb = sb("u1", [P, KC, RANK])
        v1_sb = sb("v1", [2 * RANK, FF])
        u2_sb = sb("u2", [P, FB, RANK])
        v2_sb = sb("v2", [2 * RANK, D])
        b1_col = sb("b1_col", [P, FB])
        bo_rows, b2_rows = sb("bo_rows", [P, RT, D]), sb("b2_rows", [P, RT, D])
        eps = sb("eps", [P, RT])
        minus_half = sb("minus_half", [P, RT])
        sums = sb("sums", [P, 2, N])
        recip = sb("recip", [P, 2, N])
        raw, rcp = two(sb, "raw", [P, KC, N]), two(sb, "rcp", [P, KC, N])
        attn = two(sb, "attn", [P, KC, N])
        x_sb = two(sb, "x", [P, RT, D])
        y_sb = two(sb, "y", [P, RT, D])
        y_b2 = two(sb, "y_b2", [P, RT, D])
        res = sb("res", [P, RT, D])
        o_sb = two(sb, "o", [P, RT, D])
        stats = two(sb, "stats", [P, RT, 6])
        mean_var = two(sb, "mean_var", [P, RT, 2])
        var_eps = two(sb, "var_eps", [P, RT])
        rstd = two(sb, "rstd", [P, RT])
        yT = sb("yT", [P, KC, N])
        low1 = sb("low1", [2 * RANK, HN])
        hT = sb("hT", [P, FB, N])
        low2 = sb("low2", [2 * RANK, HN])
        rows_ps = ps("rows_ps", [P, RT * D])
        low1_ps, low2_ps = ps("low1_ps", [P, N]), ps("low2_ps", [P, N])
        h_ps = two(ps, "h_ps", [P, 2, N])
        yT_ps = h_ps[0]

        constants_in = sem("constants_in")
        const_set = sem("const_set")
        sums_in = sem("sums_in")
        recip_made = sem("recip_made")
        recip_stored = sem("recip_stored")
        block_in = two(sem, "block_in")
        bo_added = sem("bo_added")
        divided = sem("divided")
        projected = sem("projected")
        x_added = sem("x_added")
        stat_made = two(sem, "stat_made")
        stat_seen = sem("stat_seen")
        var_made = two(sem, "var_made")
        eps_added = two(sem, "eps_added")
        rstd_made = two(sem, "rstd_made")
        y_made = sem("y_made")
        b2_added = sem("b2_added")
        turned = sem("turned")
        yT_copied = sem("yT_copied")
        low1_made = sem("low1_made")
        low1_copied = sem("low1_copied")
        h_made = sem("h_made")
        gelu_done = sem("gelu_done")
        low2_made = sem("low2_made")
        low2_copied = sem("low2_copied")
        ffn_made = sem("ffn_made")
        res_made = sem("res_made")
        o_seen = sem("o_seen")
        o_made = sem("o_made")
        stored = two(sem, "stored")

        CONSTANTS, LOADS = 11, 5
        FP = FB // 2

        block = ctx.enter_context(nc.Block())

        def count(b, j, per=1, start=0):
            return b * (NB * per) + ((j + 1) * per + start)

        def parity_count(b, j, per):
            return b * (NB // 2 * per) + (j // 2 + 1) * per

        def run_blocks(eng, period):
            with eng.Fori(0, B - 1) as b:
                for j in range(NB):
                    period(b, j, 2)
            for j in range(NB):
                period(B - 1, j, NB - 1 - j)

        @block.sync
        def _(sp):
            def load(b, j):
                b, j, done = b + j // NB, j % NB, block_in[j % 2]
                for c in range(KC):
                    heads = out_raw[bass.ds(b * H + c * HH, HH), :, :]
                    sp.dma_start(raw[j % 2][:, c, :], heads[:, 32 * j:32 * j + HD, :]).then_inc(done, 16)
                    sp.dma_start(rcp[j % 2][:, c, :], recips[bass.ds(b * H + c * HH, HH), j:j + 1, :]
                                 .to_broadcast([HH, HD, N])).then_inc(done, 16)
                sp.dma_start(x_sb[j % 2][:, :, :], x[bass.ds(b, 1), j * N:(j + 1) * N, :]
                             .rearrange("a (t p) d -> p (a t) d", p=P)).then_inc(done, 16)

            sp.dma_start(sums[:, :, :], out_raw.rearrange("h (j r) n -> (h j) r n", r=32)[:, HD, :]
                         .rearrange("(p l) n -> p l n", l=2)).then_inc(sums_in, 16)
            sp.dma_start(ident[:, :], identity_in).then_inc(constants_in, 16)
            sp.dma_start(wo_sb[:, :, :], wo.rearrange("(c p) n -> p c n", p=P)).then_inc(constants_in, 16)
            sp.dma_start(u1_sb[:, :, :], u1.rearrange("(c p) n -> p c n", p=P)).then_inc(constants_in, 16)
            for a in (0, RANK):
                sp.dma_start(v1_sb[a:a + RANK, :], v1).then_inc(constants_in, 16)
                sp.dma_start(v2_sb[a:a + RANK, :], v2).then_inc(constants_in, 16)
            sp.dma_start(u2_sb[:, :, :], u2.rearrange("(f p) n -> p f n", p=P)).then_inc(constants_in, 16)
            sp.dma_start(b1_col[:, :], b1.rearrange("(f p) -> p f", p=P), allow_slow_non_contiguous=True).then_inc(constants_in, 16)
            for rows, src in ((bo_rows, bo), (b2_rows, b2)):
                sp.dma_start(rows[:, :, :], src.partition_broadcast(RT).partition_broadcast(P)).then_inc(constants_in, 16)
            sp.wait_ge(recip_made, 1)
            sp.dma_start(recips.rearrange("h j n -> (h j) n").rearrange("(p l) n -> p l n", l=2),
                         recip[:, :, :]).then_inc(recip_stored, 16)
            sp.wait_ge(recip_stored, 16)
            load(0, 0)
            load(0, 1)

            def period(b, j, ahead):
                if ahead >= 2:
                    sp.wait_ge(y_made, count(b, j))
                    load(b, j + 2)
                sp.wait_ge(o_made, count(b, j))
                sp.sem_inc(o_seen, 1)
                sp.dma_start(out[bass.ds(b, 1), j * N:(j + 1) * N, :].rearrange("a (t p) d -> p (a t) d", p=P),
                             o_sb[j % 2][:, :, :]).then_inc(stored[j % 2], 16)

            run_blocks(sp, period)
            for par in range(2):
                sp.wait_ge(stored[par], 16 * (B * NB // 2) + 16)

        @block.tensor
        def _(pe):
            def project(b, j):
                pe.wait_ge(divided, count(b, j))
                pe.wait_ge(res_made, count(b, j - 2, start=2))
                for t in range(RT):
                    for c in range(KC):
                        last = nc.tensor.matmul(rows_ps[:, t * D:(t + 1) * D], attn[j % 2][:, c, t * P:(t + 1) * P],
                                                wo_sb[:, c, :], start=(c == 0), stop=(c == KC - 1))
                last.then_inc(projected, 1)

            def turn(b, j):
                pe.wait_ge(y_made, count(b, j))
                pe.wait_ge(gelu_done, count(b, j - 1, FB, start=4))
                for c in range(KC):
                    for t in range(RT):
                        last = nc.tensor.transpose(yT_ps[:, c, t * P:(t + 1) * P],
                                                   y_sb[j % 2][:, t, c * P:(c + 1) * P], ident[:, :])
                last.then_inc(turned, 1)

            def period(b, j, ahead):
                halves = [(i, slice(i * RANK, (i + 1) * RANK), slice(i * HN, (i + 1) * HN)) for i in range(2)]
                pe.wait_ge(yT_copied, count(b, j))
                pe.wait_ge(low1_copied, count(b, j - 1, start=1))
                for c in range(KC):
                    for i, part, rows in halves:
                        last = nc.tensor.matmul(low1_ps[part, 0:HN], u1_sb[:, c, :], yT[:, c, rows],
                                                start=(c == 0), stop=(c == KC - 1))
                last.then_inc(low1_made, 1)
                if ahead >= 1:
                    project(b, j + 1)
                pe.wait_ge(low1_copied, count(b, j, start=1))
                for f in range(FB):
                    if f % 2 == 0:
                        pe.wait_ge(gelu_done, count(b, j - 1, FB, start=4) + (f - 2 if f >= 4 else 0))
                    for i, part, rows in halves:
                        last = nc.tensor.matmul(h_ps[f // 2 % 2][:, i, f % 2 * HN:(f % 2 + 1) * HN],
                                                v1_sb[part, f * P:(f + 1) * P], low1[part, :], start=True, stop=True)
                    if f % 2:
                        last.then_inc(h_made, 1)
                pe.wait_ge(low2_copied, count(b, j - 1, start=1))
                for f in range(FB):
                    pe.wait_ge(gelu_done, count(b, j - 1, FB, start=4) + (f + 1))
                    for i, part, rows in halves:
                        last = nc.tensor.matmul(low2_ps[part, 0:HN], u2_sb[:, f, :], hT[:, f, rows],
                                                start=(f == 0), stop=(f == FB - 1))
                last.then_inc(low2_made, 1)
                if ahead >= 1:
                    turn(b, j + 1)
                    pe.wait_ge(x_added, count(b, j + 1, start=1))
                else:
                    pe.wait_ge(res_made, count(b, j - 1, start=2))
                pe.wait_ge(low2_copied, count(b, j, start=1))
                for t in (0, 2, 1, 3):
                    i, part, rows = halves[t // 2]
                    last = nc.tensor.matmul(rows_ps[:, t * D:(t + 1) * D], low2[part, t % 2 * P:(t % 2 + 1) * P],
                                            v2_sb[part, :], start=True, stop=True)
                last.then_inc(ffn_made, 1)

            pe.sem_inc(low1_made, 1)
            pe.sem_inc(h_made, FP)
            pe.sem_inc(low2_made, 1)
            pe.sem_inc(ffn_made, 1)
            pe.wait_ge(constants_in, 16 * CONSTANTS)
            project(0, 0)
            turn(0, 0)
            run_blocks(pe, period)

        @block.scalar
        def _(act):
            def copy_turned(b, j):
                act.wait_ge(turned, count(b, j))
                act.wait_ge(low1_made, count(b, j - 1, start=1))
                nc.scalar.activation(yT[:, :, :], yT_ps[:, :, :], ACT.Identity).then_inc(yT_copied, 1)

            def period(b, j, ahead):
                act.wait_ge(low1_made, count(b, j, start=1))
                act.wait_ge(h_made, count(b, j - 1, FP, start=FP))
                nc.scalar.activation(low1[:, :], low1_ps[:, 0:HN], ACT.Identity).then_inc(low1_copied, 1)
                act.wait_ge(low2_made, count(b, j - 1, start=1))
                for f in range(FB):
                    act.wait_ge(h_made, count(b, j - 1, FP, start=FP) + (f // 2 + 1))
                    nc.scalar.activation(hT[:, f, :].rearrange("p (i n) -> p i n", i=2),
                                         h_ps[f // 2 % 2][:, :, f % 2 * HN:(f % 2 + 1) * HN], ACT.Gelu_apprx_tanh,
                                         bias=b1_col[:, f:f + 1]).then_inc(gelu_done, 1)
                act.wait_ge(low2_made, count(b, j, start=1))
                act.wait_ge(ffn_made, count(b, j - 1, start=1))
                nc.scalar.activation(low2[:, :], low2_ps[:, 0:HN], ACT.Identity).then_inc(low2_copied, 1)
                if ahead >= 1:
                    copy_turned(b, j + 1)

            act.sem_inc(low1_copied, 1)
            act.sem_inc(gelu_done, 4)
            act.sem_inc(low2_copied, 1)
            act.wait_ge(constants_in, 16 * CONSTANTS)
            copy_turned(0, 0)
            run_blocks(act, period)

        @block.vector
        def _(dve):
            def divide(b, j):
                dve.wait_ge(block_in[j % 2], parity_count(b, j, 16 * LOADS))
                if not (isinstance(b, int) and b == 0 and j < 2):
                    dve.wait_ge(projected, count(b, j - 2))
                nc.vector.tensor_tensor(attn[j % 2][:, :, :], raw[j % 2][:, :, :], rcp[j % 2][:, :, :],
                                        ALU.mult).then_inc(divided, 1)

            def norm(which, src, dst, b, j, done):
                for t in range(RT):
                    nc.vector.bn_stats(stats[which][:, t, :], src[:, t, :]).then_inc(stat_made[which], 1)
                dve.wait_ge(stat_made[which], count(b, j, RT))
                dve.sem_inc(stat_seen, 1)
                for t in range(RT):
                    last = nc.vector.bn_aggr(mean_var[which][:, t, :], stats[which][:, t, :])
                last.then_inc(var_made[which], 1)
                dve.wait_ge(rstd_made[which], count(b, j))
                dve.wait_ge(var_made[which], count(b, j))
                for t in range(RT):
                    last = nc.vector.tensor_scalar(dst[:, t, :], src[:, t, :], mean_var[which][:, t, 0:1],
                                                   rstd[which][:, t:t + 1], ALU.subtract, ALU.mult)
                last.then_inc(done, 1)

            def first_norm(b, j):
                dve.wait_ge(bo_added, count(b, j))
                dve.wait_ge(projected, count(b, j))
                rows = x_sb[j % 2][:, :, :].rearrange("p t d -> p (t d)")
                nc.vector.tensor_tensor(rows, rows_ps[:, :], rows, ALU.add).then_inc(x_added, 1)
                dve.wait_ge(x_added, count(b, j, start=1))
                norm(0, x_sb[j % 2], y_sb[j % 2], b, j, y_made)

            def period(b, j, ahead):
                if ahead >= 1:
                    first_norm(b, j + 1)
                else:
                    dve.wait_ge(o_made, count(b, j - 1))
                if ahead >= 2:
                    divide(b, j + 2)
                dve.wait_ge(b2_added, count(b, j))
                dve.wait_ge(ffn_made, count(b, j, start=1))
                nc.vector.tensor_tensor(res[:, :, :].rearrange("p t d -> p (t d)"), rows_ps[:, :],
                                        y_b2[j % 2][:, :, :].rearrange("p t d -> p (t d)"), ALU.add).then_inc(res_made, 1)
                dve.wait_ge(res_made, count(b, j, start=2))
                dve.wait_ge(stored[j % 2], parity_count(b, j, 16))
                norm(1, res, o_sb[j % 2], b, j, o_made)

            dve.sem_inc(x_added, 1)
            dve.sem_inc(res_made, 2)
            for par in range(2):
                dve.sem_inc(stored[par], 16)
            nc.vector.memset(minus_half[:, :], -0.5).then_inc(const_set, 1)
            nc.vector.memset(eps[:, :], EPS).then_inc(const_set, 1)
            dve.wait_ge(sums_in, 16)
            nc.vector.reciprocal(recip[:, :, :], sums[:, :, :]).then_inc(recip_made, 1)
            divide(0, 0)
            divide(0, 1)
            first_norm(0, 0)
            run_blocks(dve, period)

        @block.gpsimd
        def _(pool):
            def rstd_of(which, b, j):
                pool.wait_ge(var_made[which], count(b, j))
                nc.gpsimd.tensor_tensor(var_eps[which][:, :], mean_var[which][:, :, 1], eps[:, :],
                                        ALU.add).then_inc(eps_added[which], 1)
                pool.wait_ge(eps_added[which], count(b, j))
                nc.gpsimd.tensor_tensor(rstd[which][:, :], var_eps[which][:, :], minus_half[:, :],
                                        ALU.pow).then_inc(rstd_made[which], 1)

            def add_bo(b, j):
                pool.wait_ge(block_in[j % 2], parity_count(b, j, 16 * LOADS))
                nc.gpsimd.tensor_tensor(x_sb[j % 2][:, :, :], x_sb[j % 2][:, :, :], bo_rows[:, :, :],
                                        ALU.add).then_inc(bo_added, 1)

            def after_first_norm(b, j):
                rstd_of(0, b, j)
                pool.wait_ge(y_made, count(b, j))
                if not (isinstance(b, int) and b == 0 and j < 2):
                    pool.wait_ge(res_made, count(b, j - 2, start=2))
                nc.gpsimd.tensor_tensor(y_b2[j % 2][:, :, :], y_sb[j % 2][:, :, :], b2_rows[:, :, :],
                                        ALU.add).then_inc(b2_added, 1)

            def period(b, j, ahead):
                if ahead >= 1:
                    after_first_norm(b, j + 1)
                rstd_of(1, b, j)
                if ahead >= 2:
                    add_bo(b, j + 2)

            pool.wait_ge(constants_in, 16 * CONSTANTS)
            pool.wait_ge(const_set, 2)
            add_bo(0, 0)
            add_bo(0, 1)
            after_first_norm(0, 0)
            run_blocks(pool, period)


def build(nc, x, wq, bq, wk, bk, wv, bv, wo, bo, u1, v1, b1, u2, v2, b2, alibi_k, alibi_q, identity, identity_bf16, out):
    k_parts = nc.dram_tensor("k_parts", [BH, SPLIT_ROWS, S], BF16).ap()
    q_parts = nc.dram_tensor("q_parts", [BH, SPLIT_ROWS, S], BF16).ap()
    v_rows = nc.dram_tensor("v_rows", [BH, P, NT * VW], F32).ap()
    out_raw = nc.dram_tensor("out_raw", [BH, P, N], F32).ap()
    recips = nc.dram_tensor("recips", [BH, NB, N], F32).ap()
    project_and_split(nc, x, {"q": wq, "k": wk, "v": wv}, {"q": bq, "k": bk, "v": bv}, alibi_k, alibi_q,
                      k_parts, q_parts, v_rows, identity)
    attention(nc, k_parts, q_parts, v_rows, out_raw, identity_bf16)
    project_and_feed_forward(nc, x, out_raw, recips, wo, bo, u1, v1, b1, u2, v2, b2, identity, out)


INPUTS = ["L0_attn_x", "L0_attn_Wq", "L0_attn_bq", "L0_attn_Wk", "L0_attn_bk", "L0_attn_Wv", "L0_attn_bv",
          "L0_attn_Wo", "L0_attn_bo", "L0_ffn_U1", "L0_ffn_V1", "L0_ffn_b1", "L0_ffn_U2", "L0_ffn_V2", "L0_ffn_b2"]


def kernel(**inputs):
    import concourse.bacc as bacc
    from concourse.bass_utils import run_bass_kernel_spmd

    nc = bacc.Bacc("TRN2", target_bir_lowering=False, num_devices=1)
    alibi_k, alibi_q = alibi_rows()
    arrays = {name: np.ascontiguousarray(inputs[name]) for name in INPUTS}
    arrays |= {"alibi_k": alibi_k, "alibi_q": alibi_q, "identity": np.eye(P, dtype=np.float32),
               "identity_bf16": np.eye(P).astype(mybir.dt.np(BF16))}
    args = [nc.dram_tensor(name, a.shape, mybir.dt.from_np(a.dtype), kind="ExternalInput").ap()
            for name, a in arrays.items()]
    out = nc.dram_tensor("out", (B, S, D), F32, kind="ExternalOutput").ap()
    build(nc, *args, out)
    return run_bass_kernel_spmd(nc, [arrays], core_ids=[0]).results[0]["out"]
```

```python
from contextlib import ExitStack

import numpy as np

import concourse.bass as bass
from concourse import mybir

F32 = mybir.dt.float32
BF16 = mybir.dt.bfloat16
ALU = mybir.AluOpType
ACT = mybir.ActivationFunctionType
AX = mybir.AxisListType

P = 128
B, S, D = 4, 2048, 256
H = 16
HD = D // H
BH = B * H
KC = D // P
HH = H // KC
NT = S // P
N = 512
NB = S // N
FF, RANK = 1024, 64
EPS = 1e-5
SCALE = float(HD) ** -0.5
PARTS = 3
SPLIT_ROWS = PARTS * HD + PARTS
VW = 2 * HD


def split_constant(x):
    parts, rest = [], x.astype(np.float32)
    for _ in range(PARTS):
        part = rest.astype(mybir.dt.np(BF16))
        parts.append(part)
        rest = rest - part.astype(np.float32)
    return np.stack(parts, axis=-2)


def alibi_rows():
    slopes = (1.0 / 2.0 ** (np.arange(H, dtype=np.float32) / H)).astype(np.float32)
    ramp = slopes[:, None] * np.arange(S, dtype=np.float32)[None, :]
    return split_constant(ramp), split_constant(-ramp)


HALVES = [(n, c) for n in range(2) for c in range(KC)]


def all_stored(stores_done, batches):
    parts_stored, v_stored, alibi_stored = stores_done
    return ([(half_stored, 16 * PARTS * batches + 16) for half_stored in parts_stored] +
            [(v_stored, 16 * batches + 16), (alibi_stored, 2 * 16 * batches)])


def project_and_split(nc, outer, pairs, x, weights, biases, alibi_k, alibi_q, k_parts, q_parts, v_rows, stores_done,
                      identity_in, set_ones, load_first_heads):
    names = ("q", "k")
    parts_stored, v_stored, alibi_stored = stores_done
    with ExitStack() as ctx:
        def sb(name, shape, dt=F32):
            return ctx.enter_context(nc.sbuf_tensor("a_" + name, shape, dt))

        def sem(name):
            return outer.enter_context(nc.semaphore("a_" + name))

        ident = sb("ident", [P, P])
        w_sb = {n: sb("w" + n, [P, KC, D]) for n in "qkv"}
        bias_col = {n: sb("bias_" + n, [P, KC]) for n in names}
        bq_scaled = sb("bq_scaled", [P, KC])
        bv_rows = sb("bv_rows", [P, D])
        x_sb = sb("x", [P, NT, D])
        xT = sb("xT", [P, KC, S])
        full = sb("full", [P, 2, N])
        rest = sb("rest", [P, 2, N])
        parts = {n: sb("parts_" + n, [P, KC, PARTS, S], BF16) for n in names}
        v_sb = sb("v", [P, H, NT, VW])
        banks = [pairs[i // 2][:, i % 2 * N:(i % 2 + 1) * N] for i in range(8)]

        constants_in = sem("constants_in")
        ident_in = sem("ident_in")
        x_in = [sem(f"x_in{i}") for i in range(4)]
        bias_scaled = sem("bias_scaled")
        ones_set = sem("ones_set")
        transposed = sem("transposed")
        xT_ready = sem("xT_ready")
        projected = sem("projected")
        part1_out = sem("part1_out")
        rest_ready = sem("rest_ready")
        part2_out = sem("part2_out")
        split_seen = sem("split_seen")
        split_done = sem("split_done")
        v_projected = sem("v_projected")
        v_copied = sem("v_copied")
        v_ready = sem("v_ready")

        XG = KC * NB
        QK = 2 * KC * NB
        VG = NT // 2
        tiles = [(n, c, j) for n, c in HALVES for j in range(NB)]

        def value_tile(bank, t):
            for h in range(KC):
                last = nc.tensor.matmul(bank[:, t % 2 * D:(t % 2 + 1) * D], xT[:, h, t * P:(t + 1) * P],
                                        w_sb["v"][:, h, :], start=(h == 0), stop=(h == KC - 1))
            return last

        def by_head(rows):
            return rows.rearrange("p (h d) -> p h d", h=H)

        def last_value_tile(pe, t):
            i = t // 2
            if t % 2 == 0 and i >= 4:
                pe.wait_ge(v_copied, i - 3)
            last = value_tile(banks[4 + i % 4], t)
            if t % 2:
                last.then_inc(v_projected, 1)

        def free_last_value_banks(pe):
            pe.wait_ge(v_copied, VG)

        def copy_last_values(act, v_banks):
            for i in v_banks:
                act.wait_ge(v_projected, (B - 1) * VG + i + 1)
                for t in range(2):
                    last = nc.scalar.activation(v_sb[:, :, 2 * i + t, 0:HD],
                                                by_head(banks[4 + i % 4][:, t * D:(t + 1) * D]), ACT.Identity)
                last.then_inc(v_copied, 1)

        def add_last_bias(pool, v_banks):
            for i in v_banks:
                pool.wait_ge(v_copied, i + 1)
                for t in range(2 * i, 2 * i + 2):
                    last = nc.gpsimd.tensor_tensor(v_sb[:, :, t, 0:HD], v_sb[:, :, t, 0:HD], by_head(bv_rows[:, :]), ALU.add)
                last.then_inc(v_ready, 1)

        def store_values(sp, b):
            sp.wait_ge(v_ready, b * VG + 2 * VG)
            sp.dma_start(v_rows[bass.ds(b * H, H), :, :].rearrange("h p n -> p h n"),
                         v_sb[:, :, :, :].rearrange("p h t w -> p h (t w)")).then_inc(v_stored, 16)

        block = ctx.enter_context(nc.Block())

        @block.sync
        def _(sp):
            def load_x(b):
                for t in range(0, NT, NT // 4):
                    rows = slice(t * P, (t + NT // 4) * P)
                    sp.dma_start(x_sb[:, t:t + NT // 4, :], x[bass.ds(b, 1), rows, :].rearrange("a (t p) d -> p (a t) d", p=P)).then_inc(x_in[t * 4 // NT], 16)

            sp.dma_start(ident[:, :], identity_in).then_inc(ident_in, 16)
            load_x(0)
            for n in "qkv":
                sp.dma_start(w_sb[n][:, :, :], weights[n].rearrange("(c p) n -> p c n", p=P)).then_inc(constants_in, 16)
            for n in names:
                sp.dma_start(bias_col[n][:, :], biases[n].rearrange("(c p) -> p c", p=P),
                             allow_slow_non_contiguous=True).then_inc(constants_in, 16)
            sp.dma_start(bv_rows[:, :], biases["v"].partition_broadcast(P)).then_inc(constants_in, 16)

            def store(b, more=True):
                if more:
                    sp.wait_ge(transposed, b * XG + XG)
                    load_x(b + 1)
                    for src, dst in ((alibi_q, q_parts), (alibi_k, k_parts)):
                        sp.dma_start(dst[bass.ds((b + 1) * H, H), PARTS * HD:SPLIT_ROWS, :], src).then_inc(alibi_stored, 16)
                for i, (n, c) in enumerate(HALVES):
                    sp.wait_ge(split_done, b * QK + (i + 1) * NB)
                    sp.sem_inc(split_seen, 1)
                    for j in range(PARTS):
                        sp.dma_start((q_parts, k_parts)[n][bass.ds(b * H + c * HH, HH), j * HD:(j + 1) * HD, :],
                                     parts[names[n]][:, c, j, :]).then_inc(parts_stored[i], 16)
                if more:
                    sp.wait_ge(ones_set, 1)
                    store_values(sp, b)

            for src, dst in ((alibi_q, q_parts), (alibi_k, k_parts)):
                sp.dma_start(dst[0:H, PARTS * HD:SPLIT_ROWS, :], src).then_inc(alibi_stored, 16)
            with sp.Fori(0, B - 1) as b:
                store(b)
            for done, value in all_stored(stores_done, B - 1):
                sp.wait_ge(done, value)
            load_first_heads(sp)
            store(B - 1, more=False)

        @block.tensor
        def _(pe):
            pe.wait_ge(ident_in, 16)
            def transpose_and_project(b):
                g = 0
                for j in range(NB):
                    pe.wait_ge(x_in[j], b * 16 + 16)
                    for c in range(KC):
                        pe.wait_ge(v_ready, b * VG + (g + 1))
                        for i in range(NB):
                            last = nc.tensor.transpose(banks[g][:, i * P:(i + 1) * P],
                                                       x_sb[:, j * 4 + i, c * P:(c + 1) * P], ident[:, :])
                        last.then_inc(transposed, 1)
                        g += 1
                pe.wait_ge(constants_in, 16 * 6)
                for i, (n, c, j) in enumerate(tiles):
                    if n == c == 0:
                        pe.wait_ge(xT_ready, b * XG + (j + 1) * KC)
                    if i >= 8:
                        pe.wait_ge(part1_out, b * QK + i - 7)
                    for h in range(KC):
                        last = nc.tensor.matmul(banks[i % 8][:, :], w_sb[names[n]][:, h, c * P:(c + 1) * P],
                                                xT[:, h, j * N:(j + 1) * N], start=(h == 0), stop=(h == KC - 1))
                    last.then_inc(projected, 1)

            with pe.Fori(0, B - 1) as b:
                transpose_and_project(b)
                for t in range(NT):
                    if t % 2 == 0:
                        pe.wait_ge(part1_out, b * QK + (QK - 7 + t // 2))
                    last = value_tile(banks[t // 2 % 8], t)
                    if t % 2:
                        last.then_inc(v_projected, 1)
            transpose_and_project(B - 1)
            pe.wait_ge(part1_out, B * QK)
            for t in range(NT // 2):
                last_value_tile(pe, t)

        @block.scalar
        def _(act):
            for half_stored in parts_stored:
                act.sem_inc(half_stored, 16)
            act.wait_ge(constants_in, 16 * 6)
            nc.scalar.mul(bq_scaled[:, :], bias_col["q"][:, :], SCALE).then_inc(bias_scaled, 1)
            act.wait_ge(bias_scaled, 1)
            with act.Fori(0, B) as b:
                for i, (n, c, j) in enumerate(tiles):
                    if j == 0:
                        act.wait_ge(parts_stored[HALVES.index((n, c))], b * (16 * PARTS) + 16)
                    act.wait_ge(projected, b * QK + (i + 1))
                    if i >= 2:
                        act.wait_ge(split_done, b * QK + (i - 1))
                    bias = bq_scaled if n == 0 else bias_col["k"]
                    scale = SCALE if n == 0 else 1.0
                    nc.scalar.activation(full[:, i % 2, :], banks[i % 8][:, :], ACT.Identity,
                                         bias=bias[:, c:c + 1], scale=scale)
                    nc.scalar.activation(parts[names[n]][:, c, 0, j * N:(j + 1) * N], banks[i % 8][:, :], ACT.Identity,
                                         bias=bias[:, c:c + 1], scale=scale).then_inc(part1_out, 1)
            act.wait_ge(v_stored, 16 * (B - 1) + 16)
            copy_last_values(act, range(VG // 2))

        @block.vector
        def _(dve):
            def copy_and_split(b):
                g = 0
                for j in range(NB):
                    for c in range(KC):
                        dve.wait_ge(transposed, b * XG + (g + 1))
                        nc.vector.tensor_copy(xT[:, c, j * N:(j + 1) * N], banks[g][:, :]).then_inc(xT_ready, 1)
                        g += 1
                for i, (n, c, j) in enumerate(tiles):
                    dst = parts[names[n]]
                    cols = slice(j * N, (j + 1) * N)
                    dve.wait_ge(part1_out, b * QK + (i + 1))
                    nc.vector.tensor_tensor(rest[:, i % 2, :], full[:, i % 2, :], dst[:, c, 0, cols],
                                            ALU.subtract).then_inc(rest_ready, 1)
                    dve.wait_ge(rest_ready, b * QK + (i + 1))
                    nc.vector.tensor_copy(dst[:, c, 1, cols], rest[:, i % 2, :]).then_inc(part2_out, 1)
                    dve.wait_ge(part2_out, b * QK + (i + 1))
                    nc.vector.tensor_tensor(dst[:, c, 2, cols], rest[:, i % 2, :], dst[:, c, 1, cols],
                                            ALU.subtract).then_inc(split_done, 1)

            dve.sem_inc(v_ready, VG)
            dve.sem_inc(v_stored, 16)
            with dve.Fori(0, B - 1) as b:
                copy_and_split(b)
                dve.wait_ge(v_stored, b * 16 + 16)
                dve.wait_ge(constants_in, 16 * 6)
                for i in range(VG):
                    dve.wait_ge(v_projected, b * VG + (i + 1))
                    for t in range(2):
                        last = nc.vector.tensor_tensor(v_sb[:, :, 2 * i + t, 0:HD],
                                                       by_head(banks[i % 8][:, t * D:(t + 1) * D]),
                                                       by_head(bv_rows[:, :]), ALU.add)
                    last.then_inc(v_ready, 1)
            copy_and_split(B - 1)

        @block.gpsimd
        def _(pool):
            nc.gpsimd.memset(v_sb[:, :, :, HD:VW], 1.0).then_inc(ones_set, 1)
            set_ones(pool)
            pool.wait_ge(constants_in, 16 * 6)
            add_last_bias(pool, range(VG // 2))

    return {"value_tile": last_value_tile, "free_banks": free_last_value_banks,
            "copy_values": lambda act: copy_last_values(act, range(VG // 2, VG)),
            "add_bias": lambda pool: add_last_bias(pool, range(VG // 2, VG)), "store_values": lambda sp: store_values(sp, B - 1)}


SKEW = 3
R1 = 3 * HD + 2 * PARTS
R2 = 6 * HD + 3 * PARTS
RM = R2 - PARTS
CHUNK = 2 * N
CH = NT * (S // CHUNK)
LAG = 2
PR = 4
XB = 3
BLOCKS = NT * NB


def attention(nc, ctx, pairs, k_parts, q_parts, v_rows, stores_done, out_raw, identity_in):
    def sb(name, shape, dt=F32):
        return ctx.enter_context(nc.sbuf_tensor("b_" + name, shape, dt))

    def sem(name):
        return ctx.enter_context(nc.semaphore("b_" + name))

    def two(make, name, *args):
        return [make(f"{name}{i}", *args) for i in range(2)]

    q1, k1 = two(sb, "q1_", [P, S], BF16), two(sb, "k1_", [P, S], BF16)
    q2, k2 = two(sb, "q2_", [P, S], BF16), two(sb, "k2_", [P, S], BF16)
    v2 = two(sb, "v_", [P, NT, VW])
    probs = sb("probs", [P, PR, S])
    chunk_max = two(sb, "chunk_max", [P, CH])
    neg_max = two(sb, "neg_max", [P, NT])
    neg_rest = two(sb, "neg_rest", [P, NT])
    zeros = sb("zeros", [P, NT])
    neg_parts = two(sb, "neg_parts", [P, P], BF16)
    neg_rows = two(sb, "neg_rows", [PARTS * NT, P], BF16)
    ident = sb("ident", [P, P], BF16)
    out_sb = two(sb, "out_", [P, N])
    scores1 = pairs[0:2]
    scores2 = [pairs[2 + i // 2][:, i % 2 * N:(i % 2 + 1) * N] for i in range(XB)]
    out_ps = pairs[3][:, N:2 * N]

    ones_set = sem("ones_set")
    pool_cleared = sem("pool_cleared")
    pass1_in = two(sem, "pass1_in")
    pass2_in = two(sem, "pass2_in")
    max_in = two(sem, "max_in")
    chunk_made = sem("chunk_made")
    chunk_read = sem("chunk_read")
    negated = sem("negated")
    part_split = sem("part_split")
    max_split = sem("max_split")
    max_turned = sem("max_turned")
    max_ready = sem("max_ready")
    ident_in = sem("ident_in")
    block_made = sem("block_made")
    exp_done = sem("exp_done")
    probs_used = sem("probs_used")
    out_copied = sem("out_copied")
    out_stored = two(sem, "out_stored")

    LOADS1, LOADS2, LOADSM = 12, 7, 1
    PROJECT_AT, TURN_BLOCK_AT = 9, 14
    TURN_AT = 2

    def landed(base, k, loads):
        if isinstance(base, int):
            return ((base + k) // 2 + 1) * 16 * loads
        return base * (8 * loads) + ((k + 1) // 2 * 2 + 1) * (8 * loads)

    def of_head(parts, head):
        return parts[bass.ds(head, 1), :, :].rearrange("a r s -> (a r) s")

    def load_pass1(sp, head, par):
        q, k, done = of_head(q_parts, head), of_head(k_parts, head), pass1_in[par]
        for a in (0, 64):
            sp.dma_start(q1[par][a:a + 2 * HD, :], q[0:HD, :].partition_broadcast(2)).then_inc(done, 16)
            sp.dma_start(q1[par][a + 2 * HD:a + 3 * HD, :], q[HD:2 * HD, :]).then_inc(done, 16)
            sp.dma_start(q1[par][a + 3 * HD + PARTS:a + R1, :], q[3 * HD:SPLIT_ROWS, :]).then_inc(done, 16)
            sp.dma_start(k1[par][a:a + 2 * HD, :], k[0:2 * HD, :]).then_inc(done, 16)
            sp.dma_start(k1[par][a + 2 * HD:a + 3 * HD, :], k[0:HD, :]).then_inc(done, 16)
            sp.dma_start(k1[par][a + 3 * HD:a + 3 * HD + PARTS, :], k[3 * HD:SPLIT_ROWS, :]).then_inc(done, 16)

    def load_pass2(sp, head, par):
        q, k, done = of_head(q_parts, head), of_head(k_parts, head), pass2_in[par]
        two_at, one_at = SPLIT_ROWS, SPLIT_ROWS + 2 * HD
        sp.dma_start(q2[par][0:3 * HD, :], q[0:HD, :].partition_broadcast(3)).then_inc(done, 16)
        sp.dma_start(q2[par][two_at:one_at, :], q[HD:2 * HD, :].partition_broadcast(2)).then_inc(done, 16)
        sp.dma_start(q2[par][one_at:RM, :], q[2 * HD:SPLIT_ROWS, :]).then_inc(done, 16)
        sp.dma_start(k2[par][0:SPLIT_ROWS, :], k).then_inc(done, 16)
        sp.dma_start(k2[par][two_at:one_at, :], k[0:2 * HD, :]).then_inc(done, 16)
        sp.dma_start(k2[par][one_at:one_at + HD, :], k[0:HD, :]).then_inc(done, 16)
        sp.dma_start(v2[par][:, :, :].rearrange("p t w -> p (t w)"),
                     v_rows[bass.ds(head, 1), :, :].rearrange("a p n -> (a p) n")).then_inc(done, 16)

    def set_ones(pool):
        for operand in (*q1, *k1, *q2, *k2):
            nc.gpsimd.memset(operand[:, :], 1.0).then_inc(ones_set, 1)

    def load_first_heads(sp):
        sp.wait_ge(ones_set, 8)
        load_pass1(sp, 0, 0)
        load_pass1(sp, 1, 1)
        load_pass2(sp, 0, 0)

    def run(last_phase, next_phase):
        with nc.Block() as block:
            @block.sync
            def _(sp):
                def load_max(par):
                    sp.dma_start(q2[par][RM:RM + PARTS, :].rearrange("j (t q) -> j t q", q=P), neg_rows[par][:, :]).then_inc(max_in[par], 16)

                def period(base, k, ahead=2):
                    head, par = base + k, (base + k) % 2 if isinstance(base, int) else (k + 1) % 2
                    if ahead >= 2:
                        sp.wait_ge(chunk_made, (head + 1) * CH)
                        load_pass1(sp, head + 2, par)
                    if ahead >= 1:
                        sp.wait_ge(probs_used, head * NT + PR)
                        load_pass2(sp, head + 1, 1 - par)
                        sp.wait_ge(max_ready, head + 2)
                        load_max(1 - par)
                    sp.wait_ge(out_copied, head + 1)
                    sp.dma_start(out_raw[bass.ds(head, 1), :, :].rearrange("a p n -> (a p) n"),
                                 out_sb[par][:, :]).then_inc(out_stored[par], 16)

                sp.dma_start(ident[:, :], identity_in).then_inc(ident_in, 16)
                last_phase["store_values"](sp)
                for done, value in all_stored(stores_done, B):
                    sp.wait_ge(done, value)
                next_phase["load_constants"](sp)
                sp.wait_ge(max_ready, 1)
                load_max(0)
                period(0, 0)
                with sp.Fori(1, BH - 3, 2) as base:
                    period(base, 0)
                    period(base, 1)
                period(BH - 3, 0)
                for par in range(2):
                    sp.wait_ge(out_stored[par], 16 * ((BH - H) // 2) + 16)
                next_phase["load_sums"](sp)
                period(BH - 2, 0, ahead=1)
                next_phase["load_blocks"](sp)
                period(BH - 1, 0, ahead=0)

            @block.tensor
            def _(pe):
                def pass1_chunk(base, k, par, c):
                    t, keys = c // 2, c % 2 * CHUNK
                    if c == 0:
                        pe.wait_ge(pass1_in[par], landed(base, k, LOADS1))
                    if c == TURN_AT + 1 and not (isinstance(base, int) and base + k == 0):
                        pe.wait_ge(max_ready, base + k)
                    pe.wait_ge(chunk_read, (base + k) * CH + (c + 1))
                    for i, a in enumerate((0, 64)):
                        last = nc.tensor.matmul(scores1[c % 2][:, i * N:(i + 1) * N], q1[par][a:a + R1, t * P:(t + 1) * P],
                                                k1[par][a:a + R1, keys + i * N:keys + (i + 1) * N], start=True, stop=True)
                    last.then_inc(chunk_made, 1)

                def turn_max(base, k, par):
                    pe.wait_ge(max_split, base + k + 1)
                    last = isinstance(base, int) and base + k == BH - 1
                    pe.wait_ge(chunk_read, (base + k + 1) * CH + (2 if last else TURN_AT + 2))
                    nc.tensor.transpose(scores1[(TURN_AT + 1) % 2][:, :].bitcast(BF16)[:, 0:P],
                                        neg_parts[par][:, :], ident[:, :]).then_inc(max_turned, 1)

                def pass2_block(base, k, par, t, j):
                    b = t * NB + j
                    if b == 0:
                        pe.wait_ge(pass2_in[par], landed(base, k, LOADS2))
                        pe.wait_ge(max_in[par], landed(base, k, LOADSM))
                    before = b - XB if b >= XB else ((-2, -1, -3), (-3, -2, -1))[par][b]
                    pe.wait_ge(exp_done, (base + k) * BLOCKS + (before + 1 + XB))
                    nc.tensor.matmul(scores2[(b + par) % XB][:, :], k2[par][0:R2, t * P:(t + 1) * P],
                                     q2[par][0:R2, j * N:(j + 1) * N], start=True, stop=True).then_inc(block_made, 1)

                def values(base, k, par, t):
                    pe.wait_ge(exp_done, (base + k) * BLOCKS + ((t + 1) * NB + XB))
                    if t == 0 and not (isinstance(base, int) and base + k == 0):
                        pe.wait_ge(out_copied, base + k)
                    for j in range(NB):
                        last = nc.tensor.matmul(out_ps[32 * j:32 * j + VW, :], v2[par][:, t, :],
                                                probs[:, t % PR, j * N:(j + 1) * N], start=(t == 0), stop=(t == NT - 1))
                    last.then_inc(probs_used, 1)

                def period(base, k, ahead=2):
                    par = (base + k) % 2 if isinstance(base, int) else (k + 1) % 2

                    def ahead_chunk(c):
                        beyond, c = divmod(c + 2 * SKEW, CH)
                        if 1 + beyond <= ahead:
                            pass1_chunk(base, k + 1 + beyond, (par + 1 + beyond) % 2, c)

                    for t in range(NT):
                        ahead_chunk(2 * t)
                        pass2_block(base, k, par, t, 0)
                        pass2_block(base, k, par, t, 1)
                        if 2 * (t + SKEW) == CH + TURN_AT and ahead >= 1:
                            turn_max(base, k + 1, 1 - par)
                        if t >= LAG:
                            values(base, k, par, t - LAG)
                        elif not (isinstance(base, int) and base + k == 0):
                            values(base, k - 1, 1 - par, NT + t - LAG)
                        ahead_chunk(2 * t + 1)
                        pass2_block(base, k, par, t, 2)
                        pass2_block(base, k, par, t, 3)
                        if ahead == 0 and t == PROJECT_AT:
                            next_phase["project"](pe)
                        if ahead == 0 and t == TURN_BLOCK_AT:
                            next_phase["turn"](pe)

                pe.sem_inc(probs_used, PR)
                for c in range(CH):
                    pass1_chunk(0, 0, 0, c)
                    if c < NT // 2:
                        last_phase["value_tile"](pe, NT // 2 + c)
                last_phase["free_banks"](pe)
                pe.wait_ge(ident_in, 16)
                for c in range(2 * SKEW):
                    pass1_chunk(0, 1, 1, c)
                    if c == TURN_AT:
                        turn_max(0, 0, 0)
                period(0, 0)
                with pe.Fori(1, BH - 3, 2) as base:
                    period(base, 0)
                    period(base, 1)
                period(BH - 3, 0)
                period(BH - 2, 0, ahead=1)
                period(BH - 1, 0, ahead=0)
                for t in range(NT - LAG, NT):
                    values(BH - 1, 0, 1, t)

            @block.scalar
            def _(act):
                def copy_out(base, k):
                    par = (base + k) % 2 if isinstance(base, int) else (k + 1) % 2
                    act.wait_ge(probs_used, (base + k + 1) * NT + PR)
                    act.wait_ge(out_stored[par], landed(base, k, 1))
                    nc.scalar.copy(out_sb[par][:, :], out_ps[:, :]).then_inc(out_copied, 1)

                def copy_max(base, k, par):
                    act.wait_ge(max_turned, base + k + 1)
                    nc.scalar.copy(neg_rows[par][:, :], scores1[(TURN_AT + 1) % 2][:, :].bitcast(BF16)[0:PARTS * NT, 0:P]).then_inc(max_ready, 1)

                def head(base, k, last=False):
                    par = (base + k) % 2 if isinstance(base, int) else (k + 1) % 2
                    for t in range(NT):
                        act.wait_ge(probs_used, (base + k) * NT + (t + 1))
                        for j in range(NB):
                            b = t * NB + j
                            act.wait_ge(block_made, (base + k) * BLOCKS + (b + 1))
                            nc.scalar.activation(probs[:, t % PR, j * N:(j + 1) * N], scores2[(b + par) % XB][:, :],
                                                 ACT.Exp).then_inc(exp_done, 1)
                            if b == LAG * NB - 3 and not (isinstance(base, int) and base + k == 0):
                                copy_out(base, k - 1)
                            if 2 * (t + SKEW) == CH + TURN_AT and j == 0 and not last:
                                copy_max(base, k + 1, 1 - par)
                    if last:
                        next_phase["copy_turned"](act)

                act.sem_inc(exp_done, XB)
                for par in range(2):
                    act.sem_inc(out_stored[par], 16)
                last_phase["copy_values"](act)
                copy_max(0, 0, 0)
                head(0, 0)
                with act.Fori(1, BH - 1, 2) as base:
                    head(base, 0)
                    head(base, 1)
                head(BH - 1, 0, last=True)
                copy_out(BH - 1, 0)

            @block.vector
            def _(dve):
                def parity(base, k):
                    return (base + k) % 2 if isinstance(base, int) else (k + 1) % 2

                def negate(base, k):
                    par = parity(base, k)
                    dve.wait_ge(chunk_read, (base + k + 1) * CH + 2)
                    nc.vector.tensor_reduce(neg_max[par][:, :], chunk_max[par][:, :].rearrange("p (t c) -> p t c", c=2),
                                            AX.X, ALU.max, negate=True).then_inc(negated, 1)

                def head(base, k):
                    par = parity(base, k)
                    for c in range(CH):
                        dve.wait_ge(chunk_made, (base + k) * CH + (c + 1))
                        nc.vector.tensor_reduce(chunk_max[par][:, c:c + 1], scores1[c % 2][:, :], AX.X, ALU.max).then_inc(chunk_read, 1)
                        if c == 0 and not (isinstance(base, int) and base + k == 0):
                            negate(base, k - 1)

                dve.sem_inc(chunk_read, 2)
                head(0, 0)
                with dve.Fori(1, BH - 1, 2) as base:
                    head(base, 0)
                    head(base, 1)
                head(BH - 1, 0)
                negate(BH - 1, 0)
                next_phase["divide_and_norm"](dve)

            @block.gpsimd
            def _(pool):
                def split(base, k):
                    par = (base + k) % 2 if isinstance(base, int) else (k + 1) % 2
                    whole, rest, parts = neg_max[par], neg_rest[par], neg_parts[par]
                    pool.wait_ge(negated, base + k + 1)
                    nc.gpsimd.tensor_tensor(parts[:, 0:NT], whole[:, :], zeros[:, :], ALU.add).then_inc(part_split, 1)
                    pool.wait_ge(part_split, (base + k) * 3 + 1)
                    nc.gpsimd.tensor_tensor(rest[:, :], whole[:, :], parts[:, 0:NT], ALU.subtract).then_inc(part_split, 1)
                    pool.wait_ge(part_split, (base + k) * 3 + 2)
                    nc.gpsimd.tensor_tensor(parts[:, NT:2 * NT], rest[:, :], zeros[:, :], ALU.add).then_inc(part_split, 1)
                    pool.wait_ge(part_split, (base + k) * 3 + 3)
                    nc.gpsimd.tensor_tensor(parts[:, 2 * NT:3 * NT], rest[:, :], parts[:, NT:2 * NT], ALU.subtract).then_inc(max_split, 1)

                nc.gpsimd.memset(zeros[:, :], 0.0).then_inc(pool_cleared, 1)
                for par in range(2):
                    nc.gpsimd.memset(neg_parts[par][:, :], 0.0).then_inc(pool_cleared, 1)
                last_phase["add_bias"](pool)
                pool.wait_ge(pool_cleared, 3)
                split(0, 0)
                with pool.Fori(1, BH - 1, 2) as base:
                    split(base, 0)
                    split(base, 1)
                split(BH - 1, 0)
                next_phase["finish_norm"](pool)

    return set_ones, load_first_heads, out_stored, run


EARLY = (BH - H) * NB
FB = FF // P
RT = N // P
HN = N // 2


def project_and_feed_forward(nc, ctx, pairs, x, out_raw, out_stored, recips, wo, bo, u1, v1, b1, u2, v2, b2, identity_in, out):
    def sb(name, shape, dt=F32):
        return ctx.enter_context(nc.sbuf_tensor("c_" + name, shape, dt))

    def sem(name):
        return ctx.enter_context(nc.semaphore("c_" + name))

    def two(make, name, *args):
        return [make(f"{name}{i}", *args) for i in range(2)]

    ident = sb("ident", [P, P])
    wo_sb = sb("wo", [P, KC, D])
    u1_sb = sb("u1", [P, KC, RANK])
    v1_sb = sb("v1", [2 * RANK, FF])
    u2_sb = sb("u2", [P, FB, RANK])
    v2_sb = sb("v2", [2 * RANK, D])
    b1_col = sb("b1_col", [P, FB])
    bo_rows, b2_rows = sb("bo_rows", [P, RT, D]), sb("b2_rows", [P, RT, D])
    eps = sb("eps", [P, RT])
    minus_half = sb("minus_half", [P, RT])
    sums, last_sums = sb("sums", [EARLY // 2, 2, N]), sb("last_sums", [H * NB, N])
    recip, last_recip = sb("recip", [EARLY // 2, 2, N]), sb("last_recip", [H * NB, N])
    raw, rcp = two(sb, "raw", [P, KC, N]), two(sb, "rcp", [P, KC, N])
    attn = two(sb, "attn", [P, KC, N])
    x_sb = two(sb, "x", [P, RT, D])
    y_sb = two(sb, "y", [P, RT, D])
    y_b2 = two(sb, "y_b2", [P, RT, D])
    res = sb("res", [P, RT, D])
    o_sb = two(sb, "o", [P, RT, D])
    stats = two(sb, "stats", [P, RT, 6])
    mean_var = two(sb, "mean_var", [P, RT, 2])
    var_eps = two(sb, "var_eps", [P, RT])
    rstd = two(sb, "rstd", [P, RT])
    yT = sb("yT", [P, KC, N])
    low1 = sb("low1", [2 * RANK, HN])
    hT = sb("hT", [P, FB, N])
    low2 = sb("low2", [2 * RANK, HN])
    rows_ps = pairs[0]
    h_ps = [pair[:, :].rearrange("p (i n) -> p i n", i=2) for pair in pairs[1:3]]
    low1_ps, low2_ps = pairs[3][:, 0:N], pairs[3][:, N:2 * N]
    yT_ps = h_ps[0]

    constants_in = sem("constants_in")
    const_set = sem("const_set")
    sums_in = sem("sums_in")
    recip_made = sem("recip_made")
    recip_stored = sem("recip_stored")
    block_in = two(sem, "block_in")
    bo_added = sem("bo_added")
    divided = sem("divided")
    projected = sem("projected")
    x_added = sem("x_added")
    stat_made = two(sem, "stat_made")
    stat_seen = sem("stat_seen")
    var_made = two(sem, "var_made")
    eps_added = two(sem, "eps_added")
    rstd_made = two(sem, "rstd_made")
    y_made = sem("y_made")
    b2_added = sem("b2_added")
    turned = sem("turned")
    yT_copied = sem("yT_copied")
    low1_made = sem("low1_made")
    low1_copied = sem("low1_copied")
    h_made = sem("h_made")
    gelu_done = sem("gelu_done")
    low2_made = sem("low2_made")
    low2_copied = sem("low2_copied")
    ffn_made = sem("ffn_made")
    res_made = sem("res_made")
    o_seen = sem("o_seen")
    o_made = sem("o_made")
    stored = two(sem, "stored")

    sum_rows = out_raw.rearrange("h (j r) n -> (h j) r n", r=32)[:, HD, :]
    recip_rows = recips.rearrange("h j n -> (h j) n")
    CONSTANTS, LOADS = 11, 5
    FP = FB // 2

    def count(b, j, per=1, start=0):
        return b * (NB * per) + ((j + 1) * per + start)

    def parity_count(b, j, per):
        return b * (NB // 2 * per) + (j // 2 + 1) * per

    def run_blocks(eng, period):
        with eng.Fori(0, B - 1) as b:
            for j in range(NB):
                period(b, j, 2)
        for j in range(NB):
            period(B - 1, j, NB - 1 - j)

    def load(sp, b, j):
        b, j, done = b + j // NB, j % NB, block_in[j % 2]
        for c in range(KC):
            heads = out_raw[bass.ds(b * H + c * HH, HH), :, :]
            sp.dma_start(raw[j % 2][:, c, :], heads[:, 32 * j:32 * j + HD, :]).then_inc(done, 16)
            sp.dma_start(rcp[j % 2][:, c, :], recips[bass.ds(b * H + c * HH, HH), j:j + 1, :]
                         .to_broadcast([HH, HD, N])).then_inc(done, 16)
        sp.dma_start(x_sb[j % 2][:, :, :], x[bass.ds(b, 1), j * N:(j + 1) * N, :]
                     .rearrange("a (t p) d -> p (a t) d", p=P)).then_inc(done, 16)

    def load_constants(sp):
        sp.dma_start(ident[:, :], identity_in).then_inc(constants_in, 16)
        sp.dma_start(wo_sb[:, :, :], wo.rearrange("(c p) n -> p c n", p=P)).then_inc(constants_in, 16)
        sp.dma_start(u1_sb[:, :, :], u1.rearrange("(c p) n -> p c n", p=P)).then_inc(constants_in, 16)
        for a in (0, RANK):
            sp.dma_start(v1_sb[a:a + RANK, :], v1).then_inc(constants_in, 16)
            sp.dma_start(v2_sb[a:a + RANK, :], v2).then_inc(constants_in, 16)
        sp.dma_start(u2_sb[:, :, :], u2.rearrange("(f p) n -> p f n", p=P)).then_inc(constants_in, 16)
        sp.dma_start(b1_col[:, :], b1.rearrange("(f p) -> p f", p=P), allow_slow_non_contiguous=True).then_inc(constants_in, 16)
        for rows, src in ((bo_rows, bo), (b2_rows, b2)):
            sp.dma_start(rows[:, :, :], src.partition_broadcast(RT).partition_broadcast(P)).then_inc(constants_in, 16)

    def project(pe, b, j):
        pe.wait_ge(divided, count(b, j))
        for t in range(RT):
            if t % 2 == 0:
                pe.wait_ge(res_made, count(b, j - 2, 2, start=4) - (1 - t // 2))
            for c in range(KC):
                last = nc.tensor.matmul(rows_ps[:, t * D:(t + 1) * D], attn[j % 2][:, c, t * P:(t + 1) * P],
                                        wo_sb[:, c, :], start=(c == 0), stop=(c == KC - 1))
        last.then_inc(projected, 1)

    def turn(pe, b, j):
        pe.wait_ge(y_made, count(b, j))
        pe.wait_ge(gelu_done, count(b, j - 1, FB, start=4))
        for c in range(KC):
            for t in range(RT):
                last = nc.tensor.transpose(yT_ps[:, c, t * P:(t + 1) * P],
                                           y_sb[j % 2][:, t, c * P:(c + 1) * P], ident[:, :])
        last.then_inc(turned, 1)

    def copy_turned(act, b, j):
        act.wait_ge(turned, count(b, j))
        act.wait_ge(low1_made, count(b, j - 1, start=1))
        nc.scalar.activation(yT[:, :, :], yT_ps[:, :, :], ACT.Identity).then_inc(yT_copied, 1)

    def divide(dve, b, j):
        dve.wait_ge(block_in[j % 2], parity_count(b, j, 16 * LOADS))
        if not (isinstance(b, int) and b == 0 and j < 2):
            dve.wait_ge(projected, count(b, j - 2))
        nc.vector.tensor_tensor(attn[j % 2][:, :, :], raw[j % 2][:, :, :], rcp[j % 2][:, :, :],
                                ALU.mult).then_inc(divided, 1)

    def norm(dve, which, src, dst, b, j, done):
        for t in range(RT):
            nc.vector.bn_stats(stats[which][:, t, :], src[:, t, :]).then_inc(stat_made[which], 1)
        dve.wait_ge(stat_made[which], count(b, j, RT))
        dve.sem_inc(stat_seen, 1)
        for t in range(RT):
            last = nc.vector.bn_aggr(mean_var[which][:, t, :], stats[which][:, t, :])
        last.then_inc(var_made[which], 1)
        dve.wait_ge(rstd_made[which], count(b, j))
        dve.wait_ge(var_made[which], count(b, j))
        for t in range(RT):
            last = nc.vector.tensor_scalar(dst[:, t, :], src[:, t, :], mean_var[which][:, t, 0:1],
                                           rstd[which][:, t:t + 1], ALU.subtract, ALU.mult)
        last.then_inc(done, 1)

    def first_norm(dve, b, j):
        dve.wait_ge(bo_added, count(b, j))
        dve.wait_ge(projected, count(b, j))
        rows = x_sb[j % 2][:, :, :].rearrange("p t d -> p (t d)")
        nc.vector.tensor_tensor(rows, rows_ps[:, :], rows, ALU.add).then_inc(x_added, 1)
        dve.wait_ge(x_added, count(b, j, start=1))
        norm(dve, 0, x_sb[j % 2], y_sb[j % 2], b, j, y_made)

    def rstd_of(pool, which, b, j):
        pool.wait_ge(var_made[which], count(b, j))
        nc.gpsimd.tensor_tensor(var_eps[which][:, :], mean_var[which][:, :, 1], eps[:, :],
                                ALU.add).then_inc(eps_added[which], 1)
        pool.wait_ge(eps_added[which], count(b, j))
        nc.gpsimd.tensor_tensor(rstd[which][:, :], var_eps[which][:, :], minus_half[:, :],
                                ALU.pow).then_inc(rstd_made[which], 1)

    def add_bo(pool, b, j):
        pool.wait_ge(block_in[j % 2], parity_count(b, j, 16 * LOADS))
        nc.gpsimd.tensor_tensor(x_sb[j % 2][:, :, :], x_sb[j % 2][:, :, :], bo_rows[:, :, :],
                                ALU.add).then_inc(bo_added, 1)

    def after_first_norm(pool, b, j):
        rstd_of(pool, 0, b, j)
        pool.wait_ge(y_made, count(b, j))
        if not (isinstance(b, int) and b == 0 and j < 2):
            pool.wait_ge(res_made, count(b, j - 2, 2, start=4))
        nc.gpsimd.tensor_tensor(y_b2[j % 2][:, :, :], y_sb[j % 2][:, :, :], b2_rows[:, :, :],
                                ALU.add).then_inc(b2_added, 1)

    def load_sums(sp):
        sp.dma_start(sums[:, :, :], sum_rows[0:EARLY, :].rearrange("(p l) n -> p l n", l=2)).then_inc(sums_in, 16)

    def load_blocks(sp):
        sp.wait_ge(recip_made, 1)
        sp.dma_start(recip_rows[0:EARLY, :].rearrange("(p l) n -> p l n", l=2), recip[:, :, :]).then_inc(recip_stored, 16)
        sp.wait_ge(recip_stored, 16)
        load(sp, 0, 0)
        load(sp, 0, 1)

    def project_first(pe):
        pe.sem_inc(low1_made, 1)
        pe.sem_inc(h_made, FP)
        pe.sem_inc(gelu_done, 4)
        pe.sem_inc(low2_made, 1)
        pe.sem_inc(ffn_made, 2)
        pe.wait_ge(constants_in, 16 * CONSTANTS)
        project(pe, 0, 0)

    def copy_first_turned(act):
        act.sem_inc(low1_copied, 1)
        act.sem_inc(low2_copied, 1)
        copy_turned(act, 0, 0)

    def divide_and_norm(dve):
        dve.sem_inc(x_added, 1)
        dve.sem_inc(res_made, 4)
        for par in range(2):
            dve.sem_inc(stored[par], 16)
        nc.vector.memset(minus_half[:, :], -0.5).then_inc(const_set, 1)
        nc.vector.memset(eps[:, :], EPS).then_inc(const_set, 1)
        dve.wait_ge(sums_in, 16)
        nc.vector.reciprocal(recip[:, :, :], sums[:, :, :]).then_inc(recip_made, 1)
        divide(dve, 0, 0)
        divide(dve, 0, 1)
        first_norm(dve, 0, 0)

    def finish_norm(pool):
        pool.wait_ge(constants_in, 16 * CONSTANTS)
        pool.wait_ge(const_set, 2)
        add_bo(pool, 0, 0)
        add_bo(pool, 0, 1)
        after_first_norm(pool, 0, 0)

    early = {"load_constants": load_constants, "load_sums": load_sums, "load_blocks": load_blocks,
             "project": project_first, "turn": lambda pe: turn(pe, 0, 0), "copy_turned": copy_first_turned,
             "divide_and_norm": divide_and_norm, "finish_norm": finish_norm}

    def run():
        with nc.Block() as block:
            @block.sync
            def _(sp):
                for par in range(2):
                    sp.wait_ge(out_stored[par], 16 * (BH // 2) + 16)
                sp.dma_start(last_sums[:, :], sum_rows[EARLY:, :]).then_inc(sums_in, 16)
                sp.wait_ge(recip_made, 2)
                sp.dma_start(recip_rows[EARLY:, :], last_recip[:, :]).then_inc(recip_stored, 16)
                sp.wait_ge(recip_stored, 32)

                def period(b, j, ahead):
                    if ahead >= 2:
                        sp.wait_ge(y_made, count(b, j))
                        load(sp, b, j + 2)
                    sp.wait_ge(o_made, count(b, j))
                    sp.sem_inc(o_seen, 1)
                    sp.dma_start(out[bass.ds(b, 1), j * N:(j + 1) * N, :].rearrange("a (t p) d -> p (a t) d", p=P),
                                 o_sb[j % 2][:, :, :]).then_inc(stored[j % 2], 16)

                run_blocks(sp, period)
                for par in range(2):
                    sp.wait_ge(stored[par], 16 * (B * NB // 2) + 16)

            @block.tensor
            def _(pe):
                def period(b, j, ahead):
                    halves = [(i, slice(i * RANK, (i + 1) * RANK), slice(i * HN, (i + 1) * HN)) for i in range(2)]
                    pe.wait_ge(yT_copied, count(b, j))
                    pe.wait_ge(low1_copied, count(b, j - 1, start=1))
                    for c in range(KC):
                        for i, part, rows in halves:
                            last = nc.tensor.matmul(low1_ps[part, 0:HN], u1_sb[:, c, :], yT[:, c, rows],
                                                    start=(c == 0), stop=(c == KC - 1))
                    last.then_inc(low1_made, 1)
                    if ahead >= 1:
                        project(pe, b, j + 1)
                    pe.wait_ge(low1_copied, count(b, j, start=1))
                    for f in range(FB):
                        if f % 2 == 0:
                            pe.wait_ge(gelu_done, count(b, j - 1, FB, start=4) + (f - 2 if f >= 4 else 0))
                        for i, part, rows in halves:
                            last = nc.tensor.matmul(h_ps[f // 2 % 2][:, i, f % 2 * HN:(f % 2 + 1) * HN],
                                                    v1_sb[part, f * P:(f + 1) * P], low1[part, :], start=True, stop=True)
                        if f % 2:
                            last.then_inc(h_made, 1)
                    pe.wait_ge(low2_copied, count(b, j - 1, start=1))
                    for f in range(FB):
                        pe.wait_ge(gelu_done, count(b, j - 1, FB, start=4) + (f + 1))
                        for i, part, rows in halves:
                            last = nc.tensor.matmul(low2_ps[part, 0:HN], u2_sb[:, f, :], hT[:, f, rows],
                                                    start=(f == 0), stop=(f == FB - 1))
                    last.then_inc(low2_made, 1)
                    if ahead >= 1:
                        turn(pe, b, j + 1)
                        pe.wait_ge(x_added, count(b, j + 1, start=1))
                    else:
                        pe.wait_ge(res_made, count(b, j - 1, 2, start=4))
                    pe.wait_ge(low2_copied, count(b, j, start=1))
                    for t in (0, 2, 1, 3):
                        i, part, rows = halves[t // 2]
                        last = nc.tensor.matmul(rows_ps[:, t * D:(t + 1) * D], low2[part, t % 2 * P:(t % 2 + 1) * P],
                                                v2_sb[part, :], start=True, stop=True)
                        if t % 2:
                            last.then_inc(ffn_made, 1)

                run_blocks(pe, period)

            @block.scalar
            def _(act):
                def period(b, j, ahead):
                    act.wait_ge(low1_made, count(b, j, start=1))
                    act.wait_ge(h_made, count(b, j - 1, FP, start=FP))
                    nc.scalar.activation(low1[:, :], low1_ps[:, 0:HN], ACT.Identity).then_inc(low1_copied, 1)
                    act.wait_ge(low2_made, count(b, j - 1, start=1))
                    for f in range(FB):
                        act.wait_ge(h_made, count(b, j - 1, FP, start=FP) + (f // 2 + 1))
                        nc.scalar.activation(hT[:, f, :].rearrange("p (i n) -> p i n", i=2),
                                             h_ps[f // 2 % 2][:, :, f % 2 * HN:(f % 2 + 1) * HN], ACT.Gelu_apprx_tanh,
                                             bias=b1_col[:, f:f + 1]).then_inc(gelu_done, 1)
                    act.wait_ge(low2_made, count(b, j, start=1))
                    act.wait_ge(ffn_made, count(b, j - 1, 2, start=2))
                    nc.scalar.activation(low2[:, :], low2_ps[:, 0:HN], ACT.Identity).then_inc(low2_copied, 1)
                    if ahead >= 1:
                        copy_turned(act, b, j + 1)

                act.wait_ge(constants_in, 16 * CONSTANTS)
                run_blocks(act, period)

            @block.vector
            def _(dve):
                def period(b, j, ahead):
                    if ahead >= 1:
                        first_norm(dve, b, j + 1)
                    else:
                        dve.wait_ge(o_made, count(b, j - 1))
                    if ahead >= 2:
                        divide(dve, b, j + 2)
                    dve.wait_ge(b2_added, count(b, j))
                    for i, cols in enumerate((slice(0, N), slice(N, 2 * N))):
                        dve.wait_ge(ffn_made, count(b, j, 2, start=2) - (1 - i))
                        nc.vector.tensor_tensor(res[:, :, :].rearrange("p t d -> p (t d)")[:, cols], rows_ps[:, cols],
                                                y_b2[j % 2][:, :, :].rearrange("p t d -> p (t d)")[:, cols],
                                                ALU.add).then_inc(res_made, 1)
                    dve.wait_ge(res_made, count(b, j, 2, start=4))
                    dve.wait_ge(stored[j % 2], parity_count(b, j, 16))
                    norm(dve, 1, res, o_sb[j % 2], b, j, o_made)

                dve.wait_ge(sums_in, 32)
                nc.vector.reciprocal(last_recip[:, :], last_sums[:, :]).then_inc(recip_made, 1)
                run_blocks(dve, period)

            @block.gpsimd
            def _(pool):
                def period(b, j, ahead):
                    if ahead >= 1:
                        after_first_norm(pool, b, j + 1)
                    rstd_of(pool, 1, b, j)
                    if ahead >= 2:
                        add_bo(pool, b, j + 2)

                run_blocks(pool, period)

    return early, run


def build(nc, x, wq, bq, wk, bk, wv, bv, wo, bo, u1, v1, b1, u2, v2, b2, alibi_k, alibi_q, identity, identity_bf16, out):
    k_parts = nc.dram_tensor("k_parts", [BH, SPLIT_ROWS, S], BF16).ap()
    q_parts = nc.dram_tensor("q_parts", [BH, SPLIT_ROWS, S], BF16).ap()
    v_rows = nc.dram_tensor("v_rows", [BH, P, NT * VW], F32).ap()
    out_raw = nc.dram_tensor("out_raw", [BH, P, N], F32).ap()
    recips = nc.dram_tensor("recips", [BH, NB, N], F32).ap()
    with ExitStack() as ctx:
        pairs = [ctx.enter_context(nc.psum_tensor(f"pair{i}", [P, 2 * N], F32)) for i in range(4)]
        parts_stored = [ctx.enter_context(nc.semaphore(f"parts_stored{i}")) for i in range(len(HALVES))]
        stores_done = [parts_stored] + [ctx.enter_context(nc.semaphore(name)) for name in ("v_stored", "alibi_stored")]
        set_ones, load_first_heads, out_stored, attend = attention(nc, ctx, pairs, k_parts, q_parts, v_rows,
                                                                   stores_done, out_raw, identity_bf16)
        late = project_and_split(nc, ctx, pairs, x, {"q": wq, "k": wk, "v": wv}, {"q": bq, "k": bk, "v": bv}, alibi_k, alibi_q,
                          k_parts, q_parts, v_rows, stores_done, identity, set_ones, load_first_heads)
        early, finish = project_and_feed_forward(nc, ctx, pairs, x, out_raw, out_stored, recips, wo, bo, u1, v1, b1,
                                                 u2, v2, b2, identity, out)
        attend(late, early)
        finish()



INPUTS = ["L0_attn_x", "L0_attn_Wq", "L0_attn_bq", "L0_attn_Wk", "L0_attn_bk", "L0_attn_Wv", "L0_attn_bv",
          "L0_attn_Wo", "L0_attn_bo", "L0_ffn_U1", "L0_ffn_V1", "L0_ffn_b1", "L0_ffn_U2", "L0_ffn_V2", "L0_ffn_b2"]


def kernel(**inputs):
    import concourse.bacc as bacc
    from concourse.bass_utils import run_bass_kernel_spmd

    nc = bacc.Bacc("TRN2", target_bir_lowering=False, num_devices=1)
    alibi_k, alibi_q = alibi_rows()
    arrays = {name: np.ascontiguousarray(inputs[name]) for name in INPUTS}
    arrays |= {"alibi_k": alibi_k, "alibi_q": alibi_q, "identity": np.eye(P, dtype=np.float32),
               "identity_bf16": np.eye(P).astype(mybir.dt.np(BF16))}
    args = [nc.dram_tensor(name, a.shape, mybir.dt.from_np(a.dtype), kind="ExternalInput").ap()
            for name, a in arrays.items()]
    out = nc.dram_tensor("out", (B, S, D), F32, kind="ExternalOutput").ap()
    build(nc, *args, out)
    return run_bass_kernel_spmd(nc, [arrays], core_ids=[0]).results[0]["out"]
```
